# Optimizing a Trainium2 kernel written in Bass

```python
import numpy as np
import jax
import jax.numpy as jnp

def _softmax(x, axis=-1):
    return jax.nn.softmax(x, axis=axis)

def _gelu(x):
    return jax.nn.gelu(x, approximate=True)

def _silu(x):
    return jax.nn.silu(x)

def _sigmoid(x):
    return jax.nn.sigmoid(x)

def _layernorm(x, axis=-1, eps=1e-05):
    m = jnp.mean(x, axis=axis, keepdims=True)
    v = jnp.var(x, axis=axis, keepdims=True)
    return (x - m) / jnp.sqrt(v + eps)

def _scatter_add(tgt, idx, src, axis=0):
    return tgt.at[idx].add(src)

def _segment_sum(src, seg, n):
    return jax.ops.segment_sum(src, seg, n)
kernel_name = 'mk_xattn_ffn_d1_seqx_r4_184825'

def setup_inputs(seed: int=0):
    np.random.seed(seed)
    _w = jnp.asarray

    def _rec_inputs():
        import jax
        import jax.numpy as jnp
        _rk = jax.random.key(seed)
        x = -0.000125 + 0.9999 * jax.random.normal(jax.random.fold_in(_rk, 1), (2, 512, 1024), jnp.float32)
        _lenS = 512 - jax.random.randint(jax.random.fold_in(_rk, 7), (2,), 0, max(1, 512 // 4) + 1, jnp.int32)
        _lenS2 = 1024 - jax.random.randint(jax.random.fold_in(_rk, 8), (2,), 0, max(1, 1024 // 4) + 1, jnp.int32)
        _ctx_4096P = jax.random.normal(jax.random.fold_in(_rk, 11), (2, 16, 1024), jnp.float32)
        _ctx_4096c = jax.random.dirichlet(jax.random.fold_in(_rk, 511), 0.3 * jnp.ones((16,), jnp.float32), (2, 1024))
        _ctx_4096t = jnp.einsum('bsk,bkd->bsd', _ctx_4096c, _ctx_4096P)
        _ctx_4096t = _ctx_4096t * jax.lax.rsqrt(jnp.mean(jnp.square(_ctx_4096t)) + 1e-12) * 0.953939
        ctx_4096 = -5.72187e-05 + 0.999849 * (_ctx_4096t + 0.3 * jax.random.normal(jax.random.fold_in(_rk, 611), (2, 1024, 1024), jnp.float32))
        return (x, ctx_4096)
    x, ctx_4096 = _rec_inputs()

    def _L0_xattn_setup():
        import jax, jax.numpy as jnp
        import numpy as np
        QMIN = 0.0
        QMAX = 255.0

        def fake_quant(x, scale, zp):
            s = scale.reshape(())
            z = zp.reshape(())
            q = jnp.clip(jnp.round(x / s + z), QMIN, QMAX)
            return (q - z) * s
        key = jax.random.key(seed)
        k1, k2 = jax.random.split(key)
        B, M, K, N = (4, 512, 1024, 1024)
        x1 = jax.random.normal(k1, (B, M, K), dtype=jnp.float32)
        x2 = jax.random.normal(k2, (B, K, N), dtype=jnp.float32)
        x1_scale = jnp.full((1,), 8.0 / 255.0, dtype=jnp.float32)
        x1_zp = jnp.full((1,), 128.0, dtype=jnp.float32)
        x2_scale = jnp.full((1,), 8.0 / 255.0, dtype=jnp.float32)
        x2_zp = jnp.full((1,), 128.0, dtype=jnp.float32)
        return {'x1': x1, 'x2': x2, 'x1_scale': x1_scale, 'x1_zp': x1_zp, 'x2_scale': x2_scale, 'x2_zp': x2_zp}
    _L0_xattn_all = _L0_xattn_setup()
    _L0_xattn_in = {k: v for k, v in _L0_xattn_all.items() if k in ('x1_scale', 'x1_zp', 'x2_scale', 'x2_zp')}
    del _L0_xattn_all

    def _L0_ffn_setup():
        import jax, jax.numpy as jnp
        import numpy as np
        B, S, D = (4, 512, 1024)
        NUM_EXPERTS, TOP_K = (3, 2)

        def _expert_outputs(h, w1, b1, w2, b2):
            pre = jnp.einsum('bsd,edf->ebsf', h, w1) + b1[:, None, None, :]
            act = jnp.stack([jnp.tanh(pre[0]), jax.nn.gelu(pre[1], approximate=False), jax.nn.silu(pre[2])])
            return jnp.einsum('ebsf,efd->ebsd', act, w2) + b2[:, None, None, :]
        key = jax.random.key(seed)
        ks = jax.random.split(key, 8)
        scale_in = 1.0 / np.sqrt(D)
        scale_gate = 1.0 / np.sqrt(D + 1)
        return {'h': jax.random.normal(ks[0], (B, S, D), dtype=jnp.float32), 'gate_w': jax.random.uniform(ks[1], (D + 1, NUM_EXPERTS), minval=-scale_gate, maxval=scale_gate, dtype=jnp.float32), 'gate_b': jnp.zeros((NUM_EXPERTS,), dtype=jnp.float32), 'w1': jax.random.uniform(ks[2], (NUM_EXPERTS, D, D), minval=-scale_in, maxval=scale_in, dtype=jnp.float32), 'b1': jnp.zeros((NUM_EXPERTS, D), dtype=jnp.float32), 'w2': jax.random.uniform(ks[3], (NUM_EXPERTS, D, D), minval=-scale_in, maxval=scale_in, dtype=jnp.float32), 'b2': jnp.zeros((NUM_EXPERTS, D), dtype=jnp.float32)}
    _L0_ffn_all = _L0_ffn_setup()
    _L0_ffn_in = {k: v for k, v in _L0_ffn_all.items() if k in ('gate_w', 'gate_b', 'w1', 'b1', 'w2', 'b2')}
    del _L0_ffn_all
    return {'x': x, 'ctx_4096': ctx_4096, 'L0_xattn_x1_scale': _L0_xattn_in['x1_scale'], 'L0_xattn_x1_zp': _L0_xattn_in['x1_zp'], 'L0_xattn_x2_scale': _L0_xattn_in['x2_scale'], 'L0_xattn_x2_zp': _L0_xattn_in['x2_zp'], 'L0_ffn_gate_w': _L0_ffn_in['gate_w'], 'L0_ffn_gate_b': _L0_ffn_in['gate_b'], 'L0_ffn_w1': _L0_ffn_in['w1'], 'L0_ffn_b1': _L0_ffn_in['b1'], 'L0_ffn_w2': _L0_ffn_in['w2'], 'L0_ffn_b2': _L0_ffn_in['b2']}

def reference(x, ctx_4096, L0_xattn_x1_scale, L0_xattn_x1_zp, L0_xattn_x2_scale, L0_xattn_x2_zp, L0_ffn_gate_w, L0_ffn_gate_b, L0_ffn_w1, L0_ffn_b1, L0_ffn_w2, L0_ffn_b2):
    import jax
    import jax.numpy as jnp

    def _L0_xattn_ref(x1, x2, x1_scale, x1_zp, x2_scale, x2_zp):
        import jax, jax.numpy as jnp
        import numpy as np
        QMIN = 0.0
        QMAX = 255.0

        def fake_quant(x, scale, zp):
            s = scale.reshape(())
            z = zp.reshape(())
            q = jnp.clip(jnp.round(x / s + z), QMIN, QMAX)
            return (q - z) * s
        q1 = fake_quant(x1, x1_scale, x1_zp)
        q2 = fake_quant(x2, x2_scale, x2_zp)
        return jnp.matmul(q1, q2)

    def _L0_ffn_ref(h, gate_w, gate_b, w1, b1, w2, b2):
        import jax, jax.numpy as jnp
        import numpy as np
        B, S, D = (4, 512, 1024)
        NUM_EXPERTS, TOP_K = (3, 2)

        def _expert_outputs(h, w1, b1, w2, b2):
            pre = jnp.einsum('bsd,edf->ebsf', h, w1) + b1[:, None, None, :]
            act = jnp.stack([jnp.tanh(pre[0]), jax.nn.gelu(pre[1], approximate=False), jax.nn.silu(pre[2])])
            return jnp.einsum('ebsf,efd->ebsd', act, w2) + b2[:, None, None, :]
        b, s, d = h.shape
        vision_len = int(s * 0.3)
        text_strength = jnp.mean(jnp.abs(h[:, vision_len:, :]), axis=(1, 2), keepdims=True)
        vision_strength = jnp.mean(jnp.abs(h[:, :vision_len, :]), axis=(1, 2), keepdims=True)
        modality_ratio = text_strength / (vision_strength + 1e-08)
        modality_ratio = jnp.broadcast_to(modality_ratio, (b, s, 1))
        router_input = jnp.concatenate([h, modality_ratio], axis=-1)
        gate_logits = router_input @ gate_w + gate_b
        gate_scores = jax.nn.softmax(gate_logits, axis=-1)
        top_val, top_idx = jax.lax.top_k(gate_scores, TOP_K)
        top_val = top_val / (jnp.sum(top_val, axis=-1, keepdims=True) + 1e-08)
        expert_out = _expert_outputs(h, w1, b1, w2, b2)
        moe_out = jnp.zeros_like(h)
        batch_idx = jnp.arange(b)
        for i in range(TOP_K):
            j = top_idx[:, 0, i]
            out_i = expert_out[j, batch_idx]
            moe_out = moe_out + top_val[..., i:i + 1] * out_i
        return moe_out
    x = x + _L0_xattn_ref(_layernorm(x, axis=-1), ctx_4096, L0_xattn_x1_scale, L0_xattn_x1_zp, L0_xattn_x2_scale, L0_xattn_x2_zp)
    x = x + _L0_ffn_ref(_layernorm(x, axis=-1), L0_ffn_gate_w, L0_ffn_gate_b, L0_ffn_w1, L0_ffn_b1, L0_ffn_w2, L0_ffn_b2)
    return x

_drawn_inputs = setup_inputs


def setup_inputs(seed=0):
    import zlib

    import numpy as np

    out = dict(_drawn_inputs(seed))
    spreads = {'L0_ffn_gate_b': (0.0, 0.8), 'L0_ffn_b1': (0.0, 0.8), 'L0_ffn_b2': (0.0, 2.0)}
    factors = {'L0_ffn_gate_w': 8.0, 'L0_ffn_w1': 8.0, 'L0_ffn_w2': 8.0}
    for name, (base, spread) in spreads.items():
        noise = np.random.default_rng([zlib.crc32(name.encode()), seed]).standard_normal(out[name].shape)
        drawn = base * np.exp(spread * noise) if base else spread * noise
        out[name] = jnp.asarray(drawn.astype(out[name].dtype))
    for name, factor in factors.items():
        out[name] = (out[name] * factor).astype(out[name].dtype)
    return out
```

```python
from contextlib import ExitStack

import concourse.bass as bass
from concourse import mybir

B, S, D = 2, 512, 1024
KC = 1024
P = 128
NE = 3
TOP_K = 2
VISION = int(S * 0.3)
LN_EPS = 1e-5
QC = 128.0

TT = S // P
KT = D // P
H = D // 2
PAIRS = B * TOP_K
UNITS = 4
CH = 4
RAW = 8
CTXN = B * KT

ALU = mybir.AluOpType
ACT = mybir.ActivationFunctionType
AX = mybir.AxisListType
F32 = mybir.dt.float32
F32R = mybir.dt.float32r
BF16 = mybir.dt.bfloat16
U8 = mybir.dt.uint8
I32 = mybir.dt.int32

EXPERT_ACT = [ACT.Tanh, ACT.Gelu, ACT.Silu]


def build(nc, x, ctx_in, s1, z1, s2, z2, gate_w, gate_b, w1, b1, w2, b2, out):
    x_v = x.rearrange("b (t p) d -> (b t) p d", p=P)
    out_v = out.rearrange("b (t p) d -> (b t) p d", p=P)
    ctx_v = ctx_in.rearrange("b (k p) n -> (b k) p n", p=P)
    w1_v = w1.rearrange("e (k p) n -> p (e k) n", p=P)
    w2_v = w2.rearrange("e (k p) n -> p (e k) n", p=P)
    b1_v = b1.rearrange("e (f p) -> (e f) p", p=P)

    with ExitStack() as st:
        at = [(nc.sbuf_base + 63) // 64 * 64]

        def sb(name, shape, dt, offset=None):
            size = {F32: 4, F32R: 4, I32: 4, BF16: 2, U8: 1}[dt]
            for n in shape[1:]:
                size *= n
            here = at[0] if offset is None else offset
            if offset is None:
                at[0] += (size + 31) // 32 * 32
            return nc.alloc_sbuf_tensor_at(name, shape, dt, offset=here)

        def sem(name):
            return st.enter_context(nc.semaphore(name))

        w_hi, w_lo = [], []
        w_slot = []
        for i in range(2):
            w_slot.append(at[0])
            w_hi.append(sb(f"w_hi{i}", [P, KT, H], F32R))
            w_lo.append(sb(f"w_lo{i}", [P, KT, H], F32R))
        raw = sb("raw", [P, RAW, D], F32)
        xres = sb("xres", [P, B * TT, D], F32)
        hT_hi = sb("hT_hi", [P, KT, S], F32R)
        hT_lo = sb("hT_lo", [P, KT, S], F32R)
        act_at = at[0]
        act_hi = sb("act_hi", [P, KT, S], F32R)
        act_lo = sb("act_lo", [P, KT, S], F32R)
        hbuf = sb("hbuf", [P, 2, D], F32)
        b2row = hbuf[:, 0, :]
        scratch = sb("scratch", [P, 2, H], F32)
        ctxq = [sb(f"ctxq{b}", [P, KT, D], BF16, act_at + b * KT * D * 2) for b in range(B)]
        o = w_slot[1]
        q1T = sb("q1T", [P, KT, S], BF16, o); o += KT * S * 2
        q1 = sb("q1", [P, TT, D], BF16, o); o += TT * D * 2
        q1u = sb("q1u", [P, 2, D], U8, o); o += 2 * D
        ctxu = sb("ctxu", [P, 4, D], U8, o); o += 4 * D
        ybuf = sb("ybuf", [P, 2, D], F32, o); o += 2 * D * 4

        ident = sb("ident", [P, P], F32)
        ident_b = sb("ident_b", [P, P], BF16)
        ones = sb("ones", [P, P], F32)
        ones_b = sb("ones_b", [P, P], BF16)
        vis_text = sb("vis_text", [P, 2, TT], F32)
        gw = sb("gw", [P, KT, 4], F32)
        gw_hi = sb("gw_hi", [P, KT, 4], F32R)
        gw_lo = sb("gw_lo", [P, KT, 4], F32R)
        gw_last = sb("gw_last", [P, NE], F32)
        gb = sb("gb", [P, NE], F32)
        b1n = sb("b1n", [NE * KT, P], F32)
        b1T = sb("b1T", [P, NE * KT], F32)
        qp = sb("qp", [P, 4], F32)
        qc = sb("qc", [P, 8], F32)
        inv1, inv2, s12, d1, d2, c1, cd, kd = (qc[:, i:i + 1] for i in range(8))
        bn = sb("bn", [P, TT, 2, 6], F32)
        mv = sb("mv", [P, TT, 2], F32)
        var = sb("var", [P, TT], F32)
        std = sb("std", [P, TT], F32)
        rt = sb("rt", [P, 3, TT], F32)
        rstd = sb("rstd", [P, TT], F32)
        rowsum = sb("rowsum", [P, B * TT], F32)
        rterm = sb("rterm", [P, B * TT], F32)
        absum = sb("absum", [P, B * TT], F32)
        vt = sb("vt", [P, 2, TT], F32)
        vts = sb("vts", [P, 2], F32)
        ratio = sb("ratio", [P, 3], F32)
        gbias = sb("gbias", [P, NE], F32)
        lg = sb("lg", [P, NE, TT], F32)
        ex = sb("ex", [P, NE, TT], F32)
        sc = sb("sc", [P, NE, TT], F32)
        sel = sb("sel", [P, 8, TT], F32)
        pick = sb("pick", [1, 8], F32)
        expert = sb("expert", [1, PAIRS], I32)
        gate = sb("gate", [P, PAIRS * TT], F32)

        ps = st.enter_context(nc.psum_tensor("ps", [P, 8, 512], F32))

        x_in = [sem(f"x_in{i}") for i in range(B * TT)]
        raw_in = [sem(f"raw_in{i}") for i in range(RAW)]
        small_in = sem("small_in")
        b2_in = sem("b2_in")
        raw_done = sem("raw_done")
        const_ready = sem("const_ready")
        qc_ready = sem("qc_ready")
        gw_ready = sem("gw_ready")
        dve_step = sem("dve_step")
        var_ready = sem("var_ready")
        std_ready = sem("std_ready")
        q1u_ready = sem("q1u_ready")
        q1_ready = sem("q1_ready")
        q1T_ps = sem("q1T_ps")
        q1T_ready = sem("q1T_ready")
        ctxq_ready = sem("ctxq_ready")
        attn_done = sem("attn_done")
        rterm_ready = sem("rterm_ready")
        col_ready = sem("col_ready")
        xcol_ready = sem("xcol_ready")
        y_ready = sem("y_ready")
        x1_ready = sem("x1_ready")
        h_ready = sem("h_ready")
        hT_ps = sem("hT_ps")
        hT_hi_ready = sem("hT_hi_ready")
        hT_lo_ready = sem("hT_lo_ready")
        abs_ready = sem("abs_ready")
        vt_ready = sem("vt_ready")
        ratio_ps = sem("ratio_ps")
        logit_ps = sem("logit_ps")
        exp_in = sem("exp_in")
        exp_ready = sem("exp_ready")
        sel_ready = sem("sel_ready")
        b1T_ps = sem("b1T_ps")
        b1T_ready = sem("b1T_ready")
        w_hi_ready = sem("w_hi_ready")
        g1_done = sem("g1_done")
        act_ready = sem("act_ready")
        act_lo_ready = sem("act_lo_ready")
        g2_done = sem("g2_done")
        y2_done = sem("y2_done")
        b2_used = sem("b2_used")
        out_done = sem("out_done")
        SMALL = 8

        def raw_chunk(n):
            return raw[:, n, :].rearrange("p (k n) -> p k n", k=2)

        block = st.enter_context(nc.Block())

        @block.sync
        def _(sp):
            for b in range(B):
                for t in range(TT):
                    sp.dma_start(xres[:, b * TT + t, :], x_v[b * TT + t]).then_inc(x_in[b * TT + t], 16)
            for c in range(CTXN):
                if c >= RAW:
                    sp.wait_ge(raw_done, c - RAW + 1)
                sp.dma_start(raw[:, c % RAW, :], ctx_v[c]).then_inc(raw_in[c % RAW], 16)
            with sp.Fori(0, PAIRS) as p:
                sp.wait_ge(sel_ready, p + 1)
                e = sp.value_load(expert[0:1, bass.ds(p, 1)], min_val=0, max_val=NE - 1)
                for j in range(UNITS):
                    w_v = w1_v if j < 2 else w2_v
                    for g in range(CH):
                        n = CH * j + g
                        sp.wait_ge(raw_done, p * (UNITS * CH) + (CTXN + n - RAW + 1))
                        sp.dma_start(raw_chunk(n % RAW),
                                     w_v[:, bass.ds(e * KT + 2 * g, 2), (j % 2) * H:(j % 2 + 1) * H],
                                     ).then_inc(raw_in[n % RAW], 16)
                    if j == 0:
                        sp.wait_ge(b2_used, p * TT)
                        sp.dma_start(b2row, b2[bass.ds(e, 1), :].to_broadcast([P, D])).then_inc(b2_in, 16)

        @block.gpsimd
        def _(pool):
            nc.gpsimd.memset(ones[:], 1.0).then_inc(const_ready, 1)
            nc.gpsimd.memset(ones_b[:], 1.0).then_inc(const_ready, 1)
            nc.gpsimd.memset(gw[:], 0.0).then_inc(const_ready, 1)
            pool.wait_ge(const_ready, 3)
            nc.gpsimd.affine_select(out=ident[:], in_=ones[:], compare_op=ALU.is_equal, fill=0.0, base=0,
                                    pattern=[[-1, P]], channel_multiplier=1).then_inc(const_ready, 1)
            nc.gpsimd.affine_select(out=ident_b[:], in_=ones_b[:], compare_op=ALU.is_equal, fill=0.0, base=0,
                                    pattern=[[-1, P]], channel_multiplier=1).then_inc(const_ready, 1)
            nc.gpsimd.affine_select(out=vis_text[:, 0, :], in_=ones[:, 0:TT], compare_op=ALU.is_ge, fill=0.0,
                                    base=VISION - 1, pattern=[[-P, TT]], channel_multiplier=-1
                                    ).then_inc(const_ready, 1)
            nc.gpsimd.affine_select(out=vis_text[:, 1, :], in_=ones[:, 0:TT], compare_op=ALU.is_ge, fill=0.0,
                                    base=-VISION, pattern=[[P, TT]], channel_multiplier=1
                                    ).then_inc(const_ready, 1)
            for b in range(B):
                for k in range(KT):
                    c = b * KT + k
                    pool.wait_ge(raw_done, c + 1)
                    nc.gpsimd.tensor_scalar(ctxq[b][:, k, :], ctxu[:, c % 4, :], -QC, 1.0, ALU.add, ALU.mult
                                            ).then_inc(ctxq_ready, 1)
                for t in range(TT):
                    if t == 0:
                        pool.wait_ge(col_ready, 2 * b + 2)
                    pool.wait_ge(q1u_ready, b * TT + t + 1)
                    xt = xres[:, b * TT + t, :]
                    nc.gpsimd.tensor_tensor(xt, xt, scratch[:].rearrange("p a n -> p (a n)"), ALU.add
                                            ).then_inc(xcol_ready, 1)
            for b in range(B):
                for m in range(2 * TT):
                    pool.wait_ge(y2_done, (TOP_K * b + TOP_K - 1) * 2 * TT + m + 1)
                    t, c = b * TT + m % TT, (m // TT) * H
                    pool.dma_start(out_v[t, :, c:c + H], xres[:, t, c:c + H]).then_inc(out_done, 16)
            pool.wait_ge(out_done, 16 * B * 2 * TT)

        @block.scalar
        def _(act):
            with nc.allow_non_contiguous_dma(reason="small operands"):
                act.dma_start(qp[:, 0:1], s1.to_broadcast([P, 1])).then_inc(small_in, 16)
                act.dma_start(qp[:, 1:2], z1.to_broadcast([P, 1])).then_inc(small_in, 16)
                act.dma_start(qp[:, 2:3], s2.to_broadcast([P, 1])).then_inc(small_in, 16)
                act.dma_start(qp[:, 3:4], z2.to_broadcast([P, 1])).then_inc(small_in, 16)
                act.wait_ge(const_ready, 3)
                act.dma_start(gw[:, :, 0:NE], gate_w[0:D, :].rearrange("(k p) e -> p k e", p=P)
                              ).then_inc(small_in, 16)
                act.dma_start(gw_last[:], gate_w[D:D + 1, :].to_broadcast([P, NE])).then_inc(small_in, 16)
                act.dma_start(gb[:], gate_b.rearrange("(a e) -> a e", a=1).to_broadcast([P, NE])
                              ).then_inc(small_in, 16)
                act.dma_start(b1n[:], b1_v).then_inc(small_in, 16)

            def sqrt_var(i):
                act.wait_ge(var_ready, i)
                nc.scalar.activation(std[:], var[:], ACT.Sqrt).then_inc(std_ready, 1)

            def quant_ctx(c):
                act.wait_ge(raw_in[c % RAW], 16 * (c // RAW + 1))
                if c >= 4:
                    act.wait_ge(ctxq_ready, c - 3)
                nc.scalar.activation(ctxu[:, c % 4, :], raw[:, c % RAW, :], ACT.Identity,
                                     bias=qp[:, 3:4], scale=inv2).then_inc(raw_done, 1)

            def centre_q1(b, t):
                act.wait_ge(q1u_ready, b * TT + t + 1)
                if b:
                    act.wait_ge(q1T_ps, t + 1)
                nc.scalar.activation(q1[:, t, :], q1u[:, t % 2, :], ACT.Copy, bias=-QC,
                                     accum_out=rowsum[:, b * TT + t:b * TT + t + 1]).then_inc(q1_ready, 1)

            def load_q1T(b, t):
                act.wait_ge(q1T_ps, b * TT + t + 1)
                nc.scalar.activation(q1T[:, :, t * P:(t + 1) * P],
                                     ps[:, 6 + t % 2, :].bitcast(BF16).rearrange("p (k s) -> p k s", k=KT),
                                     ACT.Copy).then_inc(q1T_ready, 1)

            def col_term(b):
                act.wait_ge(attn_done, 5 * b + 3)
                if b:
                    act.wait_ge(xcol_ready, b * TT)
                    act.wait_ge(abs_ready, b * TT)
                for c in range(2):
                    nc.scalar.activation(scratch[:, c, :], ps[:, 4 + c, :], ACT.Copy, scale=c1
                                         ).then_inc(col_ready, 1)

            def attn_out(b, t):
                if t == 0:
                    act.wait_ge(rterm_ready, b + 1)
                act.wait_ge(attn_done, 5 * b + (t + 1 if t < 2 else t + 2))
                i = b * TT + t
                if i >= 2:
                    act.wait_ge(x1_ready, i - 1)
                for c in range(2):
                    nc.scalar.activation(ybuf[:, t % 2, c * H:(c + 1) * H], ps[:, 2 * (t % 2) + c, :],
                                         ACT.Identity, bias=rterm[:, i:i + 1], scale=s12).then_inc(y_ready, 1)

            def split_h(b, t):
                i = b * TT + t
                act.wait_ge(h_ready, i + 1)
                if i:
                    act.wait_ge(abs_ready, i)
                nc.scalar.activation(scratch[:].rearrange("p a n -> p (a n)"), hbuf[:, t % 2, :], ACT.Abs,
                                     accum_out=absum[:, i:i + 1]).then_inc(abs_ready, 1)
                act.wait_ge(hT_ps, i + 1)
                for c in range(2):
                    nc.scalar.activation(hT_hi[:, 4 * c:4 * c + 4, t * P:(t + 1) * P],
                                         ps[:, 4 + 2 * (t % 2) + c, :].rearrange("p (k s) -> p k s", k=4),
                                         ACT.Copy).then_inc(hT_hi_ready, 1)

            def gate_exp(b):
                act.wait_ge(exp_in, b + 1)
                nc.scalar.activation(ex[:], lg[:], ACT.Exp).then_inc(exp_ready, 1)

            act.wait_ge(qc_ready, 1)
            sqrt_var(1)
            quant_ctx(0)
            for t in range(TT):
                centre_q1(0, t)
                quant_ctx(t + 1)
                load_q1T(0, t)
            for k in range(TT + 1, KT):
                quant_ctx(k)
            sqrt_var(2)
            for t in range(TT):
                centre_q1(1, t)
            col_term(0)
            for t in range(TT):
                attn_out(0, t)
            for t in range(TT):
                load_q1T(1, t)
            sqrt_var(3)
            for t in range(TT):
                split_h(0, t)
                quant_ctx(KT + 2 * t)
                quant_ctx(KT + 2 * t + 1)
            gate_exp(0)

            def w_hi_chunk(n_of_p, p, n):
                u, g = n // CH, n % CH
                act.wait_ge(raw_in[n % RAW], p * (16 * UNITS * CH // RAW) + 16 * (CTXN // RAW + n // RAW + 1))
                if g == 0 and n_of_p is not None:
                    act.wait_ge(*n_of_p)
                nc.scalar.activation(w_hi[u % 2][:, 2 * g:2 * g + 2, :], raw_chunk(n % RAW), ACT.Copy
                                     ).then_inc(w_hi_ready, 1)

            for g in range(CH):
                w_hi_chunk(None, 0, g)
            col_term(1)
            for t in range(TT):
                attn_out(1, t)

            act.wait_ge(xcol_ready, B * TT)

            with act.Fori(0, B) as b:
                for s in range(TOP_K):
                    p = b * TOP_K + s
                    e = act.value_load(expert[0:1, bass.ds(p, 1)], min_val=0, max_val=NE - 1)
                    for ee in range(NE):
                        with act.If(e == ee):
                            for f in range(KT):
                                j, g = f // TT, f % TT
                                if j == 0:
                                    if s == 0:
                                        free = (g2_done, p * KT) if g == 0 else None
                                    else:
                                        free = (g2_done, p * KT)
                                else:
                                    free = (g1_done, p * KT + TT)
                                w_hi_chunk(free, p, CH * (j + 1) + g)
                                act.wait_ge(g1_done, p * KT + f + 1)
                                if f >= 2:
                                    act.wait_ge(act_lo_ready, p * KT + f - 1)
                                bias = b1T[:, ee * KT + f:ee * KT + f + 1]
                                nc.scalar.activation(scratch[:, f % 2, :], ps[:, f % 2, :], EXPERT_ACT[ee],
                                                     bias=bias)
                                nc.scalar.activation(act_hi[:, f, :], ps[:, f % 2, :], EXPERT_ACT[ee],
                                                     bias=bias).then_inc(act_ready, 1)
                    for g in range(CH):
                        w_hi_chunk((g1_done, p * KT + 2 * TT), p, CH * 3 + g)
                    if s == 0:
                        for g in range(CH):
                            w_hi_chunk((g2_done, p * KT + TT), p, CH * 4 + g)
                    else:
                        with act.If(b == 0):
                            sqrt_var(4)
                            for t in range(TT):
                                split_h(1, t)
                            gate_exp(1)
                            for g in range(CH):
                                w_hi_chunk((g2_done, 2 * KT - TT), 1, CH * 4 + g)

        @block.vector
        def _(dve):
            steps = [0]

            def then(ins):
                steps[0] += 1
                ins.then_inc(dve_step, 1)
                dve.wait_ge(dve_step, steps[0])

            V = nc.vector

            def tile_stats(b, t, src):
                for c in range(2):
                    last = V.bn_stats(bn[:, t, c, :], src[:, c * H:(c + 1) * H])
                then(last)
                then(V.bn_aggr(mv[:, t, :], bn[:, t].rearrange("p a s -> p (a s)")))

            def var_out():
                V.tensor_scalar(var[:], mv[:, :, 1], LN_EPS, None, ALU.add).then_inc(var_ready, 1)

            def rsqrt(i):
                dve.wait_ge(std_ready, i)
                then(V.reciprocal(rt[:, 0, :], std[:]))
                then(V.tensor_tensor(rt[:, 1, :], rt[:, 0, :], var[:], ALU.mult))
                then(V.tensor_tensor(rt[:, 2, :], rt[:, 1, :], rt[:, 0, :], ALU.mult))
                then(V.tensor_scalar(rt[:, 1, :], rt[:, 2, :], -0.5, 1.5, ALU.mult, ALU.add))
                then(V.tensor_tensor(rstd[:], rt[:, 1, :], rt[:, 0, :], ALU.mult))

            def norm(b, t, src):
                return V.tensor_scalar(hbuf[:, t % 2, :], src, mv[:, t, 0:1], rstd[:, t:t + 1],
                                       ALU.subtract, ALU.mult)

            def x_stats(b):
                for t in range(TT):
                    dve.wait_ge(x_in[b * TT + t], 16)
                    tile_stats(b, t, xres[:, b * TT + t, :])
                if b:
                    dve.wait_ge(std_ready, b)
                var_out()

            def q1_codes(b, t):
                i = b * TT + t
                then(norm(b, t, xres[:, i, :]))
                if i >= 2:
                    dve.wait_ge(q1_ready, i - 1)
                V.tensor_scalar(q1u[:, t % 2, :], hbuf[:, t % 2, :], inv1, qp[:, 1:2], ALU.mult, ALU.add
                                ).then_inc(q1u_ready, 1)

            def row_term(b):
                a = b * TT
                dve.wait_ge(q1_ready, a + TT)
                then(V.tensor_scalar(rterm[:, a:a + TT], rowsum[:, a:a + TT], d2, cd, ALU.mult, ALU.add))
                V.tensor_scalar(rterm[:, a:a + TT], rterm[:, a:a + TT], s12, None, ALU.mult
                                ).then_inc(rterm_ready, 1)

            def attn_add(b, t):
                i = b * TT + t
                dve.wait_ge(y_ready, 2 * i + 2)
                dve.wait_ge(xcol_ready, i + 1)
                V.tensor_tensor(xres[:, i, :], ybuf[:, t % 2, :], xres[:, i, :], ALU.add).then_inc(x1_ready, 1)
                dve.wait_ge(x1_ready, i + 1)
                tile_stats(b, t, xres[:, i, :])

            def h_tile(b, t):
                i = b * TT + t
                if t >= 2:
                    dve.wait_ge(hT_ps, i - 1)
                    dve.wait_ge(abs_ready, i - 1)
                norm(b, t, xres[:, i, :]).then_inc(h_ready, 1)

            def h_lo(b, t):
                i = b * TT + t
                for c in range(2):
                    dve.wait_ge(hT_hi_ready, 2 * i + c + 1)
                    V.tensor_tensor(hT_lo[:, 4 * c:4 * c + 4, t * P:(t + 1) * P],
                                    ps[:, 4 + 2 * (t % 2) + c, :].rearrange("p (k s) -> p k s", k=4),
                                    hT_hi[:, 4 * c:4 * c + 4, t * P:(t + 1) * P].bitcast(F32),
                                    ALU.subtract).then_inc(hT_lo_ready, 1)

            def choose(b):
                dve.wait_ge(abs_ready, (b + 1) * TT)
                ab = absum[:, b * TT:(b + 1) * TT]
                V.tensor_tensor(vt[:, 0, :], vis_text[:, 0, :], ab, ALU.mult).then_inc(vt_ready, 1)
                V.tensor_tensor(vt[:, 1, :], vis_text[:, 1, :], ab, ALU.mult).then_inc(vt_ready, 1)
                dve.wait_ge(ratio_ps, b + 1)
                then(V.tensor_reduce(vts[:], ps[:, 1, 0:2 * TT].rearrange("p (a t) -> p a t", a=2), AX.X, ALU.add))
                then(V.tensor_scalar(ratio[:, 0:1], vts[:, 0:1], 1.0 / (VISION * D), 1e-8, ALU.mult, ALU.add))
                then(V.reciprocal(ratio[:, 1:2], ratio[:, 0:1]))
                then(V.tensor_scalar(ratio[:, 2:3], vts[:, 1:2], 1.0 / ((S - VISION) * D), ratio[:, 1:2],
                                     ALU.mult, ALU.mult))
                then(V.scalar_tensor_tensor(out=gbias[:], in0=gw_last[:], scalar=ratio[:, 2:3], in1=gb[:],
                                            op0=ALU.mult, op1=ALU.add))
                dve.wait_ge(logit_ps, b + 1)
                lps = ps[:, 0, 0:4 * TT].rearrange("p (t e) -> p e t", e=4)
                for e in range(NE):
                    last = V.tensor_scalar(sc[:, e, :], lps[:, e, :], gbias[:, e:e + 1], None, ALU.add)
                then(last)
                top, low, mid, a, c = (sel[:, i, :] for i in range(5))
                then(V.tensor_tensor(a, sc[:, 0, :], sc[:, 1, :], ALU.max))
                then(V.tensor_tensor(top, a, sc[:, 2, :], ALU.max))
                for e in range(NE):
                    last = V.tensor_tensor(lg[:, e, :], sc[:, e, :], top, ALU.subtract)
                last.then_inc(exp_in, 1)
                dve.wait_ge(exp_ready, b + 1)
                then(V.tensor_tensor(a, ex[:, 0, :], ex[:, 1, :], ALU.add))
                then(V.tensor_tensor(c, a, ex[:, 2, :], ALU.add))
                then(V.reciprocal(a, c))
                for e in range(NE):
                    last = V.tensor_tensor(sc[:, e, :], ex[:, e, :], a, ALU.mult)
                then(last)
                V.tensor_tensor(a, sc[:, 0, :], sc[:, 1, :], ALU.max)
                then(V.tensor_tensor(c, sc[:, 0, :], sc[:, 1, :], ALU.min))
                V.tensor_tensor(top, a, sc[:, 2, :], ALU.max)
                V.tensor_tensor(low, c, sc[:, 2, :], ALU.min)
                then(V.tensor_tensor(a, a, sc[:, 2, :], ALU.min))
                then(V.tensor_tensor(mid, a, c, ALU.max))
                one = lambda i: pick[0:1, i:i + 1]
                s0 = lambda e: sc[0:1, e, 0:1]
                V.tensor_tensor(one(0), s0(0), top[0:1, 0:1], ALU.is_ge)
                V.tensor_tensor(one(1), s0(1), top[0:1, 0:1], ALU.is_ge)
                V.tensor_tensor(one(2), s0(1), low[0:1, 0:1], ALU.is_le)
                then(V.tensor_tensor(one(3), s0(2), low[0:1, 0:1], ALU.is_le))
                V.tensor_scalar(one(0), one(0), -1.0, 1.0, ALU.mult, ALU.add)
                V.tensor_scalar(one(1), one(1), -1.0, 2.0, ALU.mult, ALU.add)
                then(V.tensor_scalar(one(4), one(2), -1.0, 2.0, ALU.mult, ALU.add))
                then(V.tensor_tensor(one(5), one(0), one(1), ALU.mult))
                then(V.scalar_tensor_tensor(out=one(6), in0=one(4), scalar=one(3), in1=one(2),
                                            op0=ALU.mult, op1=ALU.add))
                then(V.tensor_tensor(one(7), one(5), one(6), ALU.add))
                V.tensor_copy(expert[0:1, 2 * b:2 * b + 1], one(5)).then_inc(sel_ready, 1)
                V.tensor_scalar(expert[0:1, 2 * b + 1:2 * b + 2], one(7), -1.0, 3.0, ALU.mult, ALU.add
                                ).then_inc(sel_ready, 1)
                then(V.tensor_tensor(a, top, mid, ALU.add))
                then(V.tensor_scalar(c, a, 1e-8, None, ALU.add))
                then(V.reciprocal(a, c))
                V.tensor_tensor(gate[:, 8 * b:8 * b + 4], top, a, ALU.mult)
                then(V.tensor_tensor(gate[:, 8 * b + 4:8 * b + 8], mid, a, ALU.mult))

            def w_lo_chunk(p, n):
                u, g = n // CH, n % CH
                dve.wait_ge(w_hi_ready, p * (UNITS * CH) + n + 1)
                V.tensor_tensor(w_lo[u % 2][:, 2 * g:2 * g + 2, :], raw_chunk(n % RAW),
                                w_hi[u % 2][:, 2 * g:2 * g + 2, :].bitcast(F32), ALU.subtract
                                ).then_inc(raw_done, 1)

            dve.wait_ge(small_in, 16 * SMALL)
            V.reciprocal(inv1, qp[:, 0:1])
            V.reciprocal(inv2, qp[:, 2:3])
            V.tensor_tensor(s12, qp[:, 0:1], qp[:, 2:3], ALU.mult)
            V.tensor_scalar(d1, qp[:, 1:2], -1.0, QC, ALU.mult, ALU.add)
            then(V.tensor_scalar(d2, qp[:, 3:4], -1.0, QC, ALU.mult, ALU.add))
            V.tensor_tensor(c1, s12, d1, ALU.mult)
            then(V.tensor_scalar(kd, d1, float(KC), None, ALU.mult))
            V.tensor_tensor(cd, kd, d2, ALU.mult).then_inc(qc_ready, 1)
            then(V.tensor_copy(gw_hi[:], gw[:]))
            V.tensor_tensor(gw_lo[:], gw[:], gw_hi[:].bitcast(F32), ALU.subtract).then_inc(gw_ready, 1)
            dve.wait_ge(b1T_ps, 1)
            V.tensor_copy(b1T[:], ps[:, 0, 0:NE * KT]).then_inc(b1T_ready, 1)

            for b in range(B):
                x_stats(b)
                rsqrt(b + 1)
                for t in range(TT):
                    q1_codes(b, t)
            row_term(0)
            row_term(1)
            for t in range(TT):
                attn_add(0, t)
            var_out()
            rsqrt(3)
            h_tile(0, 0)
            for t in range(TT):
                if t + 1 < TT:
                    h_tile(0, t + 1)
                h_lo(0, t)
            choose(0)
            for g in range(CH):
                w_lo_chunk(0, g)
            for t in range(TT):
                attn_add(1, t)
            var_out()

            with dve.Fori(0, B) as b:
                for s in range(TOP_K):
                    p = b * TOP_K + s
                    dve.wait_ge(b2_in, p * 16 + 16)
                    for f in range(KT):
                        w_lo_chunk(p, CH * (f // TT + 1) + f % TT)
                        if f < TT:
                            if f == 0:
                                dve.wait_ge(y2_done, p * KT)
                            xt = xres[:, bass.ds(b * TT + f, 1), :].rearrange("p a n -> p (a n)")
                            V.scalar_tensor_tensor(out=xt, in0=b2row, scalar=gate[:, bass.ds(p * TT + f, 1)],
                                                   in1=xt, op0=ALU.mult, op1=ALU.add).then_inc(b2_used, 1)
                        dve.wait_ge(act_ready, p * KT + f + 1)
                        V.tensor_tensor(act_lo[:, f, :], scratch[:, f % 2, :], act_hi[:, f, :].bitcast(F32),
                                        ALU.subtract).then_inc(act_lo_ready, 1)
                    dve.wait_ge(b2_used, p * TT + TT)

                    def result(m):
                        dve.wait_ge(g2_done, p * KT + m + 1)
                        c = (m // TT) * H
                        xt = xres[:, bass.ds(b * TT + m % TT, 1), c:c + H].rearrange("p a n -> p (a n)")
                        V.scalar_tensor_tensor(out=xt, in0=ps[:, 2 + m % 2, :],
                                               scalar=gate[:, bass.ds(p * TT + m % TT, 1)],
                                               in1=xt, op0=ALU.mult, op1=ALU.add).then_inc(y2_done, 1)

                    for g in range(CH):
                        w_lo_chunk(p, CH * 3 + g)
                    if s == 0:
                        for m in range(TT):
                            result(m)
                        for g in range(CH):
                            w_lo_chunk(p, CH * 4 + g)
                            result(TT + g)
                    else:
                        with dve.If(b == 0):
                            rsqrt(4)
                            h_tile(1, 0)
                        for m in range(TT):
                            with dve.If(b == 0):
                                if m + 1 < TT:
                                    h_tile(1, m + 1)
                                h_lo(1, m)
                            result(m)
                        with dve.If(b == 0):
                            choose(1)
                        for g in range(CH):
                            with dve.If(b == 0):
                                w_lo_chunk(1, CH * 4 + g)
                            result(TT + g)

        @block.tensor
        def _(pe):
            T = nc.tensor

            def transpose_q1(b, t):
                i = b * TT + t
                pe.wait_ge(q1_ready, i + 1)
                if i >= 2:
                    pe.wait_ge(q1T_ready, i - 1)
                bank = ps[:, 6 + t % 2, :].bitcast(BF16)
                for k in range(KT):
                    last = T.transpose(bank[:, k * P:(k + 1) * P], q1[:, t, k * P:(k + 1) * P], ident_b[:])
                last.then_inc(q1T_ps, 1)

            def attention(b):
                pe.wait_ge(q1T_ready, b * TT + TT)
                for k in range(KT):
                    pe.wait_ge(ctxq_ready, b * KT + k + 1)
                    for t in range(2):
                        for c in range(2):
                            last = T.matmul(ps[:, 2 * t + c, :], q1T[:, k, t * P:(t + 1) * P],
                                            ctxq[b][:, k, c * H:(c + 1) * H], start=k == 0, stop=k == KT - 1)
                        if k == KT - 1:
                            last.then_inc(attn_done, 1)
                    for c in range(2):
                        last = T.matmul(ps[:, 4 + c, :], ones_b[:], ctxq[b][:, k, c * H:(c + 1) * H],
                                        start=k == 0, stop=k == KT - 1)
                last.then_inc(attn_done, 1)
                for t in range(2, TT):
                    pe.wait_ge(y_ready, 2 * (b * TT + t - 1))
                    for k in range(KT):
                        for c in range(2):
                            last = T.matmul(ps[:, 2 * (t % 2) + c, :], q1T[:, k, t * P:(t + 1) * P],
                                            ctxq[b][:, k, c * H:(c + 1) * H], start=k == 0, stop=k == KT - 1)
                    last.then_inc(attn_done, 1)

            def transpose_h(b, t):
                i = b * TT + t
                pe.wait_ge(h_ready, i + 1)
                if t >= 2:
                    pe.wait_ge(hT_lo_ready, 2 * (i - 1))
                for k in range(KT):
                    last = T.transpose(ps[:, 4 + 2 * (t % 2) + k // 4, (k % 4) * P:(k % 4 + 1) * P],
                                       hbuf[:, t % 2, k * P:(k + 1) * P], ident[:])
                last.then_inc(hT_ps, 1)

            def gate_products(b):
                pe.wait_ge(vt_ready, 2 * b + 2)
                T.matmul(ps[:, 1, 0:2 * TT], ones[:], vt[:].rearrange("p a t -> p (a t)"), start=True, stop=True
                         ).then_inc(ratio_ps, 1)
                for t in range(TT):
                    pe.wait_ge(hT_lo_ready, 2 * (b * TT + t) + 2)
                    n = 0
                    for k in range(KT):
                        tok = slice(t * P, (t + 1) * P)
                        for h, g in ((hT_hi, gw_hi), (hT_hi, gw_lo), (hT_lo, gw_hi)):
                            last = T.matmul(ps[:, 0, 4 * t:4 * t + 4], h[:, k, tok], g[:, k, :],
                                            start=n == 0, stop=n == 3 * KT - 1)
                            n += 1
                last.then_inc(logit_ps, 1)

            pe.wait_ge(const_ready, 7)
            pe.wait_ge(small_in, 16 * SMALL)
            T.transpose(ps[:, 0, 0:NE * KT], b1n[:], ident[0:NE * KT, 0:NE * KT]).then_inc(b1T_ps, 1)
            pe.wait_ge(b1T_ready, 1)
            for t in range(TT):
                transpose_q1(0, t)
            attention(0)
            for t in range(TT):
                transpose_q1(1, t)
            pe.wait_ge(col_ready, 2)
            pe.wait_ge(q1T_ready, 2 * TT)
            for t in range(TT):
                transpose_h(0, t)
            pe.wait_ge(y_ready, 2 * TT)
            pe.wait_ge(gw_ready, 1)
            gate_products(0)
            pe.wait_ge(hT_lo_ready, 2 * TT)
            pe.wait_ge(exp_in, 1)
            attention(1)
            pe.wait_ge(y_ready, 4 * TT)

            with pe.Fori(0, B) as b:
                for s in range(TOP_K):
                    p = b * TOP_K + s
                    for f in range(KT):
                        j, g = f // TT, f % TT
                        if f >= 2:
                            pe.wait_ge(act_ready, p * KT + f - 1)
                        n = 0
                        fs = slice(g * P, (g + 1) * P)
                        for k in range(KT):
                            if g == 0 and k % 2 == 0:
                                pe.wait_ge(raw_done, p * (UNITS * CH) + (CTXN + CH * j + k // 2 + 1))
                            for w, h in ((w_hi, hT_hi), (w_hi, hT_lo), (w_lo, hT_hi)):
                                last = T.matmul(ps[:, f % 2, :], w[j][:, k, fs], h[:, k, :],
                                                start=n == 0, stop=n == 3 * KT - 1)
                                n += 1
                        last.then_inc(g1_done, 1)
                    for m in range(2 * TT):
                        j, t = m // TT, m % TT
                        if m >= 2:
                            pe.wait_ge(y2_done, p * KT + m - 1)
                        n = 0
                        tok = slice(t * P, (t + 1) * P)
                        for k in range(KT):
                            if t == 0 and k % 2 == 0:
                                pe.wait_ge(raw_done, p * (UNITS * CH) + (CTXN + CH * (2 + j) + k // 2 + 1))
                            if m == 0:
                                pe.wait_ge(act_lo_ready, p * KT + k + 1)
                            for a, w in ((act_hi, w_hi), (act_hi, w_lo), (act_lo, w_hi)):
                                last = T.matmul(ps[:, 2 + m % 2, :], a[:, k, tok], w[j][:, k, :],
                                                start=n == 0, stop=n == 3 * KT - 1)
                                n += 1
                        last.then_inc(g2_done, 1)
                        if s == 1 and m < TT:
                            with pe.If(b == 0):
                                transpose_h(1, m)
                        if s == 1 and m == TT:
                            with pe.If(b == 0):
                                gate_products(1)


_INS = ["x", "ctx_4096", "L0_xattn_x1_scale", "L0_xattn_x1_zp", "L0_xattn_x2_scale", "L0_xattn_x2_zp",
        "L0_ffn_gate_w", "L0_ffn_gate_b", "L0_ffn_w1", "L0_ffn_b1", "L0_ffn_w2", "L0_ffn_b2"]


def kernel(**inputs):
    import numpy as np
    import concourse.bacc as bacc
    from concourse.bass_utils import run_bass_kernel_spmd

    nc = bacc.Bacc("TRN2", target_bir_lowering=False, num_devices=1)
    arrays, args = {}, []
    for name in _INS:
        a = np.ascontiguousarray(inputs[name])
        arrays[f"in_{name}_dram"] = a
        args.append(nc.dram_tensor(f"in_{name}_dram", a.shape, mybir.dt.from_np(a.dtype), kind="ExternalInput").ap())
    out = nc.dram_tensor("out_0_dram", (B, S, D), F32, kind="ExternalOutput").ap()
    build(nc, *args, out)
    r = run_bass_kernel_spmd(nc, [arrays], core_ids=[0])
    return r.results[0]["out_0_dram"]
```

```python
from contextlib import ExitStack

import concourse.bass as bass
from concourse import mybir

B, S, D = 2, 512, 1024
KC = 1024
P = 128
NE = 3
TOP_K = 2
VISION = int(S * 0.3)
LN_EPS = 1e-5
QC = 128.0

TT = S // P
KT = D // P
H = D // 2
PAIRS = B * TOP_K
UNITS = 4
CH = 4
RAW = 8
CTXN = B * KT

ALU = mybir.AluOpType
ACT = mybir.ActivationFunctionType
AX = mybir.AxisListType
F32 = mybir.dt.float32
F32R = mybir.dt.float32r
BF16 = mybir.dt.bfloat16
U8 = mybir.dt.uint8
I32 = mybir.dt.int32

ATT_BANK = [0, 2, 6, 0]

EXPERT_ACT = [ACT.Tanh, ACT.Gelu, ACT.Silu]


def build(nc, x, ctx_in, s1, z1, s2, z2, gate_w, gate_b, w1, b1, w2, b2, out):
    x_v = x.rearrange("b (t p) d -> (b t) p d", p=P)
    out_v = out.rearrange("b (t p) d -> (b t) p d", p=P)
    ctx_v = ctx_in.rearrange("b (k p) n -> (b k) p n", p=P)
    w1_v = w1.rearrange("e (k p) n -> p (e k) n", p=P)
    w2_v = w2.rearrange("e (k p) n -> p (e k) n", p=P)
    b1_v = b1.rearrange("e (f p) -> (e f) p", p=P)

    with ExitStack() as st:
        at = [(nc.sbuf_base + 63) // 64 * 64]

        def sb(name, shape, dt, offset=None):
            size = {F32: 4, F32R: 4, I32: 4, BF16: 2, U8: 1}[dt]
            for n in shape[1:]:
                size *= n
            here = at[0] if offset is None else offset
            if offset is None:
                at[0] += (size + 31) // 32 * 32
            return nc.alloc_sbuf_tensor_at(name, shape, dt, offset=here)

        def sem(name):
            return st.enter_context(nc.semaphore(name))

        w_hi, w_lo = [], []
        w_slot = []
        for i in range(2):
            w_slot.append(at[0])
            w_hi.append(sb(f"w_hi{i}", [P, KT, H], F32R))
            w_lo.append(sb(f"w_lo{i}", [P, KT, H], F32R))
        raw = sb("raw", [P, RAW, D], F32)
        xres = sb("xres", [P, B * TT, D], F32)
        hT_hi = sb("hT_hi", [P, KT, S], F32R)
        hT_lo = sb("hT_lo", [P, KT, S], F32R)
        act_at = at[0]
        act_hi = sb("act_hi", [P, KT, S], F32R)
        act_lo = sb("act_lo", [P, KT, S], F32R)
        hbuf = sb("hbuf", [P, 2, D], F32)
        b2row = hbuf[:, 0, :]
        scratch = sb("scratch", [P, 2, H], F32)
        lgT = scratch[0:4, 0, :]
        ctxq = [sb(f"ctxq{b}", [P, KT, D], BF16, act_at + b * KT * D * 2) for b in range(B)]
        o = w_slot[1]
        q1T = []
        for b in range(B):
            q1T.append(sb(f"q1T{b}", [P, KT, S], BF16, o)); o += KT * S * 2
        q1 = sb("q1", [P, 2, D], BF16, o); o += 2 * D * 2
        q1u = sb("q1u", [P, 2, D], U8, o); o += 2 * D
        ctxu = sb("ctxu", [P, 2, D], U8, o); o += 2 * D
        ybuf = sb("ybuf", [P, 2, D], F32, o); o += 2 * D * 4

        ident = sb("ident", [P, P], F32)
        ident_b = sb("ident_b", [P, P], BF16)
        ones = sb("ones", [P, P], F32)
        ones_b = sb("ones_b", [P, P], BF16)
        vis_text = sb("vis_text", [P, 2, TT], F32)
        gw = sb("gw", [P, KT, 4], F32)
        gw_hi = sb("gw_hi", [P, KT, 4], F32R)
        gw_lo = sb("gw_lo", [P, KT, 4], F32R)
        gw_last = sb("gw_last", [P, NE], F32)
        gb = sb("gb", [P, NE], F32)
        b1n = sb("b1n", [NE * KT, P], F32)
        b1T = sb("b1T", [P, NE * KT], F32)
        qp = sb("qp", [P, 4], F32)
        qc = sb("qc", [P, 8], F32)
        inv1, inv2, s12, d1, d2, c1, cd, kd = (qc[:, i:i + 1] for i in range(8))
        bn = sb("bn", [P, TT, 2, 6], F32)
        mv = sb("mv", [P, TT, 2], F32)
        var = sb("var", [P, TT], F32)
        std = sb("std", [P, TT], F32)
        rt = sb("rt", [P, 3, TT], F32)
        rstd = sb("rstd", [P, TT], F32)
        rterm = sb("rterm", [P, B * TT], F32)
        absum = sb("absum", [P, B * TT], F32)
        vt = sb("vt", [P, 2, TT], F32)
        vts = sb("vts", [P, 2], F32)
        ratio = sb("ratio", [P, 3], F32)
        gbias = sb("gbias", [P, NE], F32)
        lg = sb("lg", [P, NE, TT], F32)
        ex = sb("ex", [P, NE, TT], F32)
        sc = sb("sc", [P, NE, TT], F32)
        sel = sb("sel", [P, 8, TT], F32)
        pick = sb("pick", [1, 8], F32)
        expert = sb("expert", [1, PAIRS], I32)
        gate = sb("gate", [P, PAIRS * TT], F32)

        ps = st.enter_context(nc.psum_tensor("ps", [P, 8, 512], F32))

        x_in = [sem(f"x_in{i}") for i in range(B * TT)]
        raw_in = [sem(f"raw_in{i}") for i in range(RAW)]
        small_in = sem("small_in")
        b2_in = sem("b2_in")
        raw_done = sem("raw_done")
        const_ready = sem("const_ready")
        qc_ready = sem("qc_ready")
        gw_ready = sem("gw_ready")
        rowsum_ps = sem("rowsum_ps")
        logitT_ps = sem("logitT_ps")
        logitT_ready = sem("logitT_ready")
        scales_in = sem("scales_in")
        dve_step = sem("dve_step")
        var_ready = sem("var_ready")
        std_ready = sem("std_ready")
        norm1_done = sem("norm1_done")
        q1u_ready = sem("q1u_ready")
        q1_ready = sem("q1_ready")
        q1T_ps = sem("q1T_ps")
        q1T_ready = sem("q1T_ready")
        ctxq_ready = sem("ctxq_ready")
        attn_done = sem("attn_done")
        rterm_ready = sem("rterm_ready")
        col_ready = sem("col_ready")
        xcol_ready = sem("xcol_ready")
        y_ready = sem("y_ready")
        x1_ready = sem("x1_ready")
        h_ready = sem("h_ready")
        hT_ps = sem("hT_ps")
        hT_hi_ready = sem("hT_hi_ready")
        hT_lo_ready = sem("hT_lo_ready")
        abs_ready = sem("abs_ready")
        vt_ready = sem("vt_ready")
        ratio_ps = sem("ratio_ps")
        logit_ps = sem("logit_ps")
        exp_in = sem("exp_in")
        exp_ready = sem("exp_ready")
        sel_ready = sem("sel_ready")
        b1T_ps = sem("b1T_ps")
        b1T_ready = sem("b1T_ready")
        w_hi_ready = sem("w_hi_ready")
        g1_done = sem("g1_done")
        act_ready = sem("act_ready")
        act_lo_ready = sem("act_lo_ready")
        g2_done = sem("g2_done")
        y2_done = sem("y2_done")
        b2_used = sem("b2_used")
        out_done = [sem(f"out_done{b}") for b in range(B)]
        SMALL = 4

        def raw_chunk(n):
            return raw[:, n, :].rearrange("p (k n) -> p k n", k=2)

        block = st.enter_context(nc.Block())

        def store_results(eng, b):
            for m in range(2 * TT):
                eng.wait_ge(y2_done, (TOP_K * b + TOP_K - 1) * 2 * TT + m + 1)
                t, c = b * TT + m % TT, (m // TT) * H
                eng.dma_start(out_v[t, :, c:c + H], xres[:, t, c:c + H]).then_inc(out_done[b], 16)
            eng.wait_ge(out_done[b], 16 * 2 * TT)

        @block.sync
        def _(sp):
            def load_x(b):
                for i in range(b * TT, (b + 1) * TT):
                    sp.dma_start(xres[:, i, :], x_v[i]).then_inc(x_in[i], 16)

            def load_ctx(c):
                if c >= RAW:
                    sp.wait_ge(raw_done, c - RAW + 1)
                sp.dma_start(raw[:, c % RAW, :], ctx_v[c]).then_inc(raw_in[c % RAW], 16)

            load_x(0)
            with nc.allow_non_contiguous_dma(reason="small operands"):
                for i, a in enumerate((s1, z1, s2, z2)):
                    sp.dma_start(qp[:, i:i + 1], a.to_broadcast([P, 1])).then_inc(scales_in, 16)
                load_x(1)
                for c in range(KT):
                    load_ctx(c)
                sp.wait_ge(const_ready, 3)
                sp.dma_start(gw[:, :, 0:NE], gate_w[0:D, :].rearrange("(k p) e -> p k e", p=P)
                             ).then_inc(small_in, 16)
                sp.dma_start(gw_last[:], gate_w[D:D + 1, :].to_broadcast([P, NE])).then_inc(small_in, 16)
                sp.dma_start(gb[:], gate_b.rearrange("(a e) -> a e", a=1).to_broadcast([P, NE])
                             ).then_inc(small_in, 16)
                sp.dma_start(b1n[:], b1_v).then_inc(small_in, 16)
            for c in range(KT, CTXN):
                load_ctx(c)
            with sp.Fori(0, PAIRS) as p:
                sp.wait_ge(sel_ready, p + 1)
                e = sp.value_load(expert[0:1, bass.ds(p, 1)], min_val=0, max_val=NE - 1)
                for j in range(UNITS):
                    w_v = w1_v if j < 2 else w2_v
                    for g in range(CH):
                        n = CH * j + g
                        sp.wait_ge(raw_done, p * (UNITS * CH) + (CTXN + n - RAW + 1))
                        sp.dma_start(raw_chunk(n % RAW),
                                     w_v[:, bass.ds(e * KT + 2 * g, 2), (j % 2) * H:(j % 2 + 1) * H],
                                     ).then_inc(raw_in[n % RAW], 16)
                        if n == RAW:
                          sp.dma_start(b2row, b2[bass.ds(e, 1), :].to_broadcast([P, D])).then_inc(b2_in, 16)

            store_results(sp, 1)

        @block.gpsimd
        def _(pool):
            nc.gpsimd.memset(ones[:], 1.0).then_inc(const_ready, 1)
            nc.gpsimd.memset(ones_b[:], 1.0).then_inc(const_ready, 1)
            nc.gpsimd.memset(gw[:], 0.0).then_inc(const_ready, 1)
            pool.wait_ge(const_ready, 3)
            nc.gpsimd.affine_select(out=ident[:], in_=ones[:], compare_op=ALU.is_equal, fill=0.0, base=0,
                                    pattern=[[-1, P]], channel_multiplier=1).then_inc(const_ready, 1)
            nc.gpsimd.affine_select(out=ident_b[:], in_=ones_b[:], compare_op=ALU.is_equal, fill=0.0, base=0,
                                    pattern=[[-1, P]], channel_multiplier=1).then_inc(const_ready, 1)
            nc.gpsimd.affine_select(out=vis_text[:, 0, :], in_=ones[:, 0:TT], compare_op=ALU.is_ge, fill=0.0,
                                    base=VISION - 1, pattern=[[-P, TT]], channel_multiplier=-1
                                    ).then_inc(const_ready, 1)
            nc.gpsimd.affine_select(out=vis_text[:, 1, :], in_=ones[:, 0:TT], compare_op=ALU.is_ge, fill=0.0,
                                    base=-VISION, pattern=[[P, TT]], channel_multiplier=1
                                    ).then_inc(const_ready, 1)

            def centre_ctx(c):
                pool.wait_ge(raw_done, c + 1)
                nc.gpsimd.tensor_scalar(ctxq[c // KT][:, c % KT, :], ctxu[:, c % 2, :], -QC, 1.0,
                                        ALU.add, ALU.mult).then_inc(ctxq_ready, 1)

            def centre_q1(i):
                pool.wait_ge(q1u_ready, i + 1)
                if i >= 2:
                    pool.wait_ge(q1T_ps, i - 1)
                nc.gpsimd.tensor_scalar(q1[:, i % 2, :], q1u[:, i % 2, :], -QC, 1.0,
                                        ALU.add, ALU.mult).then_inc(q1_ready, 1)

            def add_column_term(b, t):
                if t == 0:
                    pool.wait_ge(col_ready, 2 * b + 2)
                pool.wait_ge(norm1_done, b * TT + t + 1)
                xt = xres[:, b * TT + t, :]
                nc.gpsimd.tensor_tensor(xt, xt, scratch[:].rearrange("p a n -> p (a n)"), ALU.add
                                        ).then_inc(xcol_ready, 1)

            for t in range(TT):
                centre_q1(t)
            for k in range(TT):
                centre_ctx(k)
            for t in range(TT):
                centre_q1(TT + t)
                centre_ctx(TT + t)
            add_column_term(0, 0)
            add_column_term(0, 1)
            centre_ctx(KT)
            add_column_term(0, 2)
            centre_ctx(KT + 1)
            add_column_term(0, 3)
            for k in range(2, KT):
                centre_ctx(KT + k)
            for t in range(TT):
                add_column_term(1, t)
            store_results(pool, 0)

        @block.scalar
        def _(act):
            def sqrt_var(i):
                act.wait_ge(var_ready, i)
                nc.scalar.activation(std[:], var[:], ACT.Sqrt).then_inc(std_ready, 1)

            def quant_ctx(c):
                act.wait_ge(raw_in[c % RAW], 16 * (c // RAW + 1))
                if c >= 2:
                    act.wait_ge(ctxq_ready, c - 1)
                nc.scalar.activation(ctxu[:, c % 2, :], raw[:, c % RAW, :], ACT.Identity,
                                     bias=qp[:, 3:4], scale=inv2).then_inc(raw_done, 1)

            def quant_x(i):
                act.wait_ge(norm1_done, i + 1)
                if i >= 2:
                    act.wait_ge(q1_ready, i - 1)
                nc.scalar.activation(q1u[:, i % 2, :], hbuf[:, i % 2, :], ACT.Identity,
                                     bias=qp[:, 1:2], scale=inv1).then_inc(q1u_ready, 1)

            def col_term(b):
                act.wait_ge(attn_done, 5 * b + 3)
                if b:
                    act.wait_ge(xcol_ready, b * TT)
                    act.wait_ge(abs_ready, b * TT)
                for c in range(2):
                    nc.scalar.activation(scratch[:, c, :], ps[:, 4 + c, :], ACT.Copy, scale=c1
                                         ).then_inc(col_ready, 1)

            def attn_out(b, t):
                if t == 0:
                    act.wait_ge(rterm_ready, b + 1)
                act.wait_ge(attn_done, 5 * b + (t + 1 if t < 2 else t + 2))
                i = b * TT + t
                if i >= 2:
                    act.wait_ge(x1_ready, i - 1)
                for c in range(2):
                    nc.scalar.activation(ybuf[:, t % 2, c * H:(c + 1) * H], ps[:, ATT_BANK[t] + c, :],
                                         ACT.Identity, bias=rterm[:, i:i + 1], scale=s12).then_inc(y_ready, 1)

            def split_h(b, t):
                i = b * TT + t
                act.wait_ge(h_ready, i + 1)
                if i:
                    act.wait_ge(abs_ready, i)
                nc.scalar.activation(scratch[:].rearrange("p a n -> p (a n)"), hbuf[:, t % 2, :], ACT.Abs,
                                     accum_out=absum[:, i:i + 1]).then_inc(abs_ready, 1)
                act.wait_ge(hT_ps, i + 1)
                for c in range(2):
                    nc.scalar.activation(hT_hi[:, 4 * c:4 * c + 4, t * P:(t + 1) * P],
                                         ps[:, 4 + 2 * (t % 2) + c, :].rearrange("p (k s) -> p k s", k=4),
                                         ACT.Copy).then_inc(hT_hi_ready, 1)

            def gate_logits(b):
                act.wait_ge(logitT_ps, b + 1)
                nc.scalar.activation(lgT, ps[0:4, 0, :], ACT.Copy).then_inc(logitT_ready, 1)

            def gate_exp(b):
                act.wait_ge(exp_in, b + 1)
                nc.scalar.activation(ex[:], lg[:], ACT.Exp).then_inc(exp_ready, 1)

            nc.scalar.preload_act_table(ACT.Sqrt)
            act.wait_ge(qc_ready, 1)
            sqrt_var(1)
            for t in range(TT):
                quant_x(t)
            for k in range(TT):
                quant_ctx(k)
            sqrt_var(2)
            for k in range(TT, KT):
                quant_ctx(k)
            col_term(0)
            for t in range(TT):
                attn_out(0, t)
                quant_ctx(KT + t)
            sqrt_var(3)
            for t in range(TT):
                split_h(0, t)
            nc.scalar.preload_act_table(ACT.Exp)
            gate_logits(0)
            gate_exp(0)
            for k in range(TT, KT):
                quant_ctx(KT + k)

            def w_hi_chunk(n_of_p, p, n):
                u, g = n // CH, n % CH
                act.wait_ge(raw_in[n % RAW], p * (16 * UNITS * CH // RAW) + 16 * (CTXN // RAW + n // RAW + 1))
                if g == 0 and n_of_p is not None:
                    act.wait_ge(*n_of_p)
                nc.scalar.activation(w_hi[u % 2][:, 2 * g:2 * g + 2, :], raw_chunk(n % RAW), ACT.Copy
                                     ).then_inc(w_hi_ready, 1)

            for g in range(CH):
                w_hi_chunk(None, 0, g)
            col_term(1)
            for t in range(TT):
                attn_out(1, t)

            sqrt_var(4)
            act.wait_ge(xcol_ready, B * TT)
            act.wait_ge(x1_ready, B * TT)

            with act.Fori(0, B) as b:
                for s in range(TOP_K):
                    p = b * TOP_K + s
                    e = act.value_load(expert[0:1, bass.ds(p, 1)], min_val=0, max_val=NE - 1)
                    for ee in range(NE):
                        with act.If(e == ee):
                            for f in range(KT):
                                j, g = f // TT, f % TT
                                act.wait_ge(g1_done, p * KT + f + 1)
                                if f >= 2:
                                    act.wait_ge(act_lo_ready, p * KT + f - 1)
                                bias = b1T[:, ee * KT + f:ee * KT + f + 1]
                                nc.scalar.activation(scratch[:, f % 2, :], ps[:, f % 2, :], EXPERT_ACT[ee],
                                                     bias=bias)
                                nc.scalar.activation(act_hi[:, f, :], ps[:, f % 2, :], EXPERT_ACT[ee],
                                                     bias=bias).then_inc(act_ready, 1)
                                w_hi_chunk((g1_done, p * KT + (TT if j else 1)), p, CH * (j + 1) + g)
                    for g in range(CH):
                        w_hi_chunk((g1_done, p * KT + 2 * TT), p, CH * 3 + g)
                    if s == 0:
                        for g in range(CH):
                            w_hi_chunk((g2_done, p * KT + TT), p, CH * 4 + g)
                    else:
                        with act.If(b == 0):
                            for t in range(TT):
                                split_h(1, t)
                            gate_logits(1)
                            gate_exp(1)
                            for g in range(CH):
                                w_hi_chunk((g2_done, 2 * KT - TT), 1, CH * 4 + g)

        @block.vector
        def _(dve):
            steps = [0]

            def then(ins):
                steps[0] += 1
                ins.then_inc(dve_step, 1)
                dve.wait_ge(dve_step, steps[0])

            V = nc.vector

            def tile_stats(b, t, src):
                for c in range(2):
                    last = V.bn_stats(bn[:, t, c, :], src[:, c * H:(c + 1) * H])
                then(last)
                then(V.bn_aggr(mv[:, t, :], bn[:, t].rearrange("p a s -> p (a s)")))

            def var_out():
                V.tensor_scalar(var[:], mv[:, :, 1], LN_EPS, None, ALU.add).then_inc(var_ready, 1)

            def rsqrt(i):
                dve.wait_ge(std_ready, i)
                then(V.reciprocal(rt[:, 0, :], std[:]))
                then(V.tensor_tensor(rt[:, 1, :], rt[:, 0, :], var[:], ALU.mult))
                then(V.tensor_tensor(rt[:, 2, :], rt[:, 1, :], rt[:, 0, :], ALU.mult))
                then(V.tensor_scalar(rt[:, 1, :], rt[:, 2, :], -0.5, 1.5, ALU.mult, ALU.add))
                then(V.tensor_tensor(rstd[:], rt[:, 1, :], rt[:, 0, :], ALU.mult))

            def norm(b, t, src):
                return V.tensor_scalar(hbuf[:, t % 2, :], src, mv[:, t, 0:1], rstd[:, t:t + 1],
                                       ALU.subtract, ALU.mult)

            def x_stats(b, t):
                dve.wait_ge(x_in[b * TT + t], 16)
                tile_stats(b, t, xres[:, b * TT + t, :])

            def norm_x(i):
                if i >= 2:
                    dve.wait_ge(q1u_ready, i - 1)
                norm(i // TT, i % TT, xres[:, i, :]).then_inc(norm1_done, 1)

            def quant_x(i):
                dve.wait_ge(norm1_done, i + 1)
                dve.wait_ge(q1_ready, i - 1)
                V.tensor_scalar(q1u[:, i % 2, :], hbuf[:, i % 2, :], inv1, qp[:, 1:2], ALU.mult, ALU.add
                                ).then_inc(q1u_ready, 1)

            def load_q1T(i):
                b, t = i // TT, i % TT
                dve.wait_ge(q1T_ps, i + 1)
                V.tensor_copy(q1T[b][:, :, t * P:(t + 1) * P],
                              ps[:, 6, :].bitcast(BF16).rearrange("p (k s) -> p k s", k=KT)
                              ).then_inc(q1T_ready, 1)

            def row_term(b):
                a = b * TT
                dve.wait_ge(rowsum_ps, b + 1)
                then(V.tensor_scalar(rterm[:, a:a + TT], ps[:, 7, a:a + TT], d2, cd, ALU.mult, ALU.add))
                V.tensor_scalar(rterm[:, a:a + TT], rterm[:, a:a + TT], s12, None, ALU.mult
                                ).then_inc(rterm_ready, 1)

            def attn_add(b, t):
                i = b * TT + t
                dve.wait_ge(y_ready, 2 * i + 2)
                dve.wait_ge(xcol_ready, i + 1)
                V.tensor_tensor(xres[:, i, :], ybuf[:, t % 2, :], xres[:, i, :], ALU.add).then_inc(x1_ready, 1)
                dve.wait_ge(x1_ready, i + 1)
                tile_stats(b, t, xres[:, i, :])

            def h_tile(b, t):
                i = b * TT + t
                if b and t == 0:
                    dve.wait_ge(b2_used, TOP_K * TT)
                if t >= 2:
                    dve.wait_ge(hT_ps, i - 1)
                    dve.wait_ge(abs_ready, i - 1)
                norm(b, t, xres[:, i, :]).then_inc(h_ready, 1)

            def h_lo(b, t):
                i = b * TT + t
                for c in range(2):
                    dve.wait_ge(hT_hi_ready, 2 * i + c + 1)
                    V.tensor_tensor(hT_lo[:, 4 * c:4 * c + 4, t * P:(t + 1) * P],
                                    ps[:, 4 + 2 * (t % 2) + c, :].rearrange("p (k s) -> p k s", k=4),
                                    hT_hi[:, 4 * c:4 * c + 4, t * P:(t + 1) * P].bitcast(F32),
                                    ALU.subtract).then_inc(hT_lo_ready, 1)

            def choose(b):
                dve.wait_ge(abs_ready, (b + 1) * TT)
                ab = absum[:, b * TT:(b + 1) * TT]
                V.tensor_tensor(vt[:, 0, :], vis_text[:, 0, :], ab, ALU.mult).then_inc(vt_ready, 1)
                V.tensor_tensor(vt[:, 1, :], vis_text[:, 1, :], ab, ALU.mult).then_inc(vt_ready, 1)
                dve.wait_ge(ratio_ps, b + 1)
                then(V.tensor_reduce(vts[:], ps[:, 1, 0:2 * TT].rearrange("p (a t) -> p a t", a=2), AX.X, ALU.add))
                then(V.tensor_scalar(ratio[:, 0:1], vts[:, 0:1], 1.0 / (VISION * D), 1e-8, ALU.mult, ALU.add))
                then(V.reciprocal(ratio[:, 1:2], ratio[:, 0:1]))
                then(V.tensor_scalar(ratio[:, 2:3], vts[:, 1:2], 1.0 / ((S - VISION) * D), ratio[:, 1:2],
                                     ALU.mult, ALU.mult))
                then(V.scalar_tensor_tensor(out=gbias[:], in0=gw_last[:], scalar=ratio[:, 2:3], in1=gb[:],
                                            op0=ALU.mult, op1=ALU.add))
                dve.wait_ge(logit_ps, b + 1)
                lps = ps[:, 4, 0:4 * TT].rearrange("p (t e) -> p e t", e=4)
                for e in range(NE):
                    last = V.tensor_scalar(sc[:, e, :], lps[:, e, :], gbias[:, e:e + 1], None, ALU.add)
                then(last)
                top, low, mid, a, c = (sel[:, i, :] for i in range(5))
                then(V.tensor_tensor(a, sc[:, 0, :], sc[:, 1, :], ALU.max))
                then(V.tensor_tensor(top, a, sc[:, 2, :], ALU.max))
                for e in range(NE):
                    last = V.tensor_tensor(lg[:, e, :], sc[:, e, :], top, ALU.subtract)
                last.then_inc(exp_in, 1)
                dve.wait_ge(exp_ready, b + 1)
                then(V.tensor_tensor(a, ex[:, 0, :], ex[:, 1, :], ALU.add))
                then(V.tensor_tensor(c, a, ex[:, 2, :], ALU.add))
                then(V.reciprocal(a, c))
                for e in range(NE):
                    last = V.tensor_tensor(sc[:, e, :], ex[:, e, :], a, ALU.mult)
                then(last)
                V.tensor_tensor(a, sc[:, 0, :], sc[:, 1, :], ALU.max)
                then(V.tensor_tensor(c, sc[:, 0, :], sc[:, 1, :], ALU.min))
                V.tensor_tensor(top, a, sc[:, 2, :], ALU.max)
                V.tensor_tensor(low, c, sc[:, 2, :], ALU.min)
                then(V.tensor_tensor(a, a, sc[:, 2, :], ALU.min))
                then(V.tensor_tensor(mid, a, c, ALU.max))
                one = lambda i: pick[0:1, i:i + 1]
                s0 = lambda e: sc[0:1, e, 0:1]
                V.tensor_tensor(one(0), s0(0), top[0:1, 0:1], ALU.is_ge)
                V.tensor_tensor(one(1), s0(1), top[0:1, 0:1], ALU.is_ge)
                V.tensor_tensor(one(2), s0(1), low[0:1, 0:1], ALU.is_le)
                then(V.tensor_tensor(one(3), s0(2), low[0:1, 0:1], ALU.is_le))
                V.tensor_scalar(one(0), one(0), -1.0, 1.0, ALU.mult, ALU.add)
                V.tensor_scalar(one(1), one(1), -1.0, 2.0, ALU.mult, ALU.add)
                then(V.tensor_scalar(one(4), one(2), -1.0, 2.0, ALU.mult, ALU.add))
                then(V.tensor_tensor(one(5), one(0), one(1), ALU.mult))
                then(V.scalar_tensor_tensor(out=one(6), in0=one(4), scalar=one(3), in1=one(2),
                                            op0=ALU.mult, op1=ALU.add))
                then(V.tensor_tensor(one(7), one(5), one(6), ALU.add))
                V.tensor_copy(expert[0:1, 2 * b:2 * b + 1], one(5)).then_inc(sel_ready, 1)
                V.tensor_scalar(expert[0:1, 2 * b + 1:2 * b + 2], one(7), -1.0, 3.0, ALU.mult, ALU.add
                                ).then_inc(sel_ready, 1)
                then(V.tensor_tensor(a, top, mid, ALU.add))
                then(V.tensor_scalar(c, a, 1e-8, None, ALU.add))
                then(V.reciprocal(a, c))
                V.tensor_tensor(gate[:, 8 * b:8 * b + 4], top, a, ALU.mult)
                then(V.tensor_tensor(gate[:, 8 * b + 4:8 * b + 8], mid, a, ALU.mult))

            def w_lo_chunk(p, n):
                u, g = n // CH, n % CH
                dve.wait_ge(w_hi_ready, p * (UNITS * CH) + n + 1)
                V.tensor_tensor(w_lo[u % 2][:, 2 * g:2 * g + 2, :], raw_chunk(n % RAW),
                                w_hi[u % 2][:, 2 * g:2 * g + 2, :].bitcast(F32), ALU.subtract
                                ).then_inc(raw_done, 1)

            def dve_constants():
                dve.wait_ge(scales_in, 16 * 4)
                V.reciprocal(inv1, qp[:, 0:1])
                V.reciprocal(inv2, qp[:, 2:3])
                V.tensor_tensor(s12, qp[:, 0:1], qp[:, 2:3], ALU.mult)
                V.tensor_scalar(d1, qp[:, 1:2], -1.0, QC, ALU.mult, ALU.add)
                then(V.tensor_scalar(d2, qp[:, 3:4], -1.0, QC, ALU.mult, ALU.add))
                V.tensor_tensor(c1, s12, d1, ALU.mult)
                then(V.tensor_scalar(kd, d1, float(KC), None, ALU.mult))
                V.tensor_tensor(cd, kd, d2, ALU.mult).then_inc(qc_ready, 1)

            for t in range(TT):
                x_stats(0, t)
            var_out()
            dve_constants()
            rsqrt(1)
            norm_x(0)
            norm_x(1)
            norm_x(2)
            norm_x(3)
            x_stats(1, 0)
            load_q1T(0)
            x_stats(1, 1)
            load_q1T(1)
            x_stats(1, 2)
            load_q1T(2)
            x_stats(1, 3)
            load_q1T(3)
            var_out()
            rsqrt(2)
            norm_x(4)
            norm_x(5)
            quant_x(4)
            quant_x(5)
            norm_x(6)
            norm_x(7)
            quant_x(6)
            row_term(0)
            load_q1T(4)
            quant_x(7)
            load_q1T(5)
            load_q1T(6)
            load_q1T(7)
            for t in range(TT):
                attn_add(0, t)
            var_out()
            dve.wait_ge(small_in, 16 * SMALL)
            then(V.tensor_copy(gw_hi[:], gw[:]))
            V.tensor_tensor(gw_lo[:], gw[:], gw_hi[:].bitcast(F32), ALU.subtract).then_inc(gw_ready, 1)
            dve.wait_ge(b1T_ps, 1)
            V.tensor_copy(b1T[:], ps[:, 7, 64:64 + NE * KT]).then_inc(b1T_ready, 1)
            row_term(1)
            rsqrt(3)
            h_tile(0, 0)
            for t in range(TT):
                if t + 1 < TT:
                    h_tile(0, t + 1)
                h_lo(0, t)
            choose(0)
            for g in range(CH):
                w_lo_chunk(0, g)
            for t in range(TT):
                attn_add(1, t)
            var_out()
            rsqrt(4)

            with dve.Fori(0, B) as b:
                for s in range(TOP_K):
                    p = b * TOP_K + s
                    for f in range(KT):
                        dve.wait_ge(act_ready, p * KT + f + 1)
                        V.tensor_tensor(act_lo[:, f, :], scratch[:, f % 2, :], act_hi[:, f, :].bitcast(F32),
                                        ALU.subtract).then_inc(act_lo_ready, 1)
                        w_lo_chunk(p, CH * (f // TT + 1) + f % TT)
                        if f >= TT:
                            t = f - TT
                            if t == 0:
                                dve.wait_ge(b2_in, p * 16 + 16)
                                dve.wait_ge(act_lo_ready, p * KT + f)
                            xt = xres[:, bass.ds(b * TT + t, 1), :].rearrange("p a n -> p (a n)")
                            V.scalar_tensor_tensor(out=xt, in0=b2row, scalar=gate[:, bass.ds(p * TT + t, 1)],
                                                   in1=xt, op0=ALU.mult, op1=ALU.add).then_inc(b2_used, 1)

                    def result(m):
                        if m == 0:
                            dve.wait_ge(b2_used, p * TT + TT)
                        dve.wait_ge(g2_done, p * KT + m + 1)
                        c = (m // TT) * H
                        xt = xres[:, bass.ds(b * TT + m % TT, 1), c:c + H].rearrange("p a n -> p (a n)")
                        V.scalar_tensor_tensor(out=xt, in0=ps[:, 2 + m % 2, :],
                                               scalar=gate[:, bass.ds(p * TT + m % TT, 1)],
                                               in1=xt, op0=ALU.mult, op1=ALU.add).then_inc(y2_done, 1)

                    if s == 0:
                        for m in range(TT):
                            w_lo_chunk(p, CH * 3 + m)
                            result(m)
                        for g in range(CH):
                            w_lo_chunk(p, CH * 4 + g)
                            result(TT + g)
                    else:
                        with dve.If(b == 0):
                            h_tile(1, 0)
                            h_tile(1, 1)
                        w_lo_chunk(p, CH * 3)
                        result(0)
                        with dve.If(b == 0):
                            h_tile(1, 2)
                            h_lo(1, 0)
                            h_tile(1, 3)
                            h_lo(1, 1)
                        w_lo_chunk(p, CH * 3 + 1)
                        result(1)
                        with dve.If(b == 0):
                            h_lo(1, 2)
                            h_lo(1, 3)
                        w_lo_chunk(p, CH * 3 + 2)
                        w_lo_chunk(p, CH * 3 + 3)
                        result(2)
                        with dve.If(b == 0):
                            choose(1)
                        result(3)
                        for g in range(CH):
                            with dve.If(b == 0):
                                w_lo_chunk(1, CH * 4 + g)
                            result(TT + g)

        @block.tensor
        def _(pe):
            T = nc.tensor

            def transpose_q1(i):
                pe.wait_ge(q1_ready, i + 1)
                if i:
                    pe.wait_ge(q1T_ready, i)
                bank = ps[:, 6, :].bitcast(BF16)
                for k in range(KT):
                    last = T.transpose(bank[:, k * P:(k + 1) * P], q1[:, i % 2, k * P:(k + 1) * P], ident_b[:])
                last.then_inc(q1T_ps, 1)

            def row_sums(b):
                pe.wait_ge(q1T_ready, b * TT + TT)
                for t in range(TT):
                    for k in range(KT):
                        last = T.matmul(ps[:, 7, b * TT + t:b * TT + t + 1], q1T[b][:, k, t * P:(t + 1) * P],
                                        ones_b[:, 0:1], start=k == 0, stop=k == KT - 1)
                last.then_inc(rowsum_ps, 1)

            def attention(b):
                for k in range(KT):
                    pe.wait_ge(ctxq_ready, b * KT + k + 1)
                    for t in range(2):
                        for c in range(2):
                            last = T.matmul(ps[:, ATT_BANK[t] + c, :], q1T[b][:, k, t * P:(t + 1) * P],
                                            ctxq[b][:, k, c * H:(c + 1) * H], start=k == 0, stop=k == KT - 1)
                        if k == KT - 1:
                            last.then_inc(attn_done, 1)
                    for c in range(2):
                        last = T.matmul(ps[:, 4 + c, :], ones_b[:], ctxq[b][:, k, c * H:(c + 1) * H],
                                        start=k == 0, stop=k == KT - 1)
                    if k == KT - 1:
                        last.then_inc(attn_done, 1)
                    if b == 0 and k >= TT:
                        transpose_q1(k)
                for t in range(2, TT):
                    if t == 2:
                        pe.wait_ge(rterm_ready, b + 1)
                        pe.wait_ge(q1T_ready, B * TT)
                    else:
                        pe.wait_ge(y_ready, 2 * b * TT + 2)
                    for k in range(KT):
                        for c in range(2):
                            last = T.matmul(ps[:, ATT_BANK[t] + c, :], q1T[b][:, k, t * P:(t + 1) * P],
                                            ctxq[b][:, k, c * H:(c + 1) * H], start=k == 0, stop=k == KT - 1)
                    last.then_inc(attn_done, 1)

            def transpose_h(b, t):
                i = b * TT + t
                pe.wait_ge(h_ready, i + 1)
                if t >= 2:
                    pe.wait_ge(hT_lo_ready, 2 * (i - 1))
                for k in range(KT):
                    last = T.transpose(ps[:, 4 + 2 * (t % 2) + k // 4, (k % 4) * P:(k % 4 + 1) * P],
                                       hbuf[:, t % 2, k * P:(k + 1) * P], ident[:])
                last.then_inc(hT_ps, 1)

            def gate_product(b, t):
                pe.wait_ge(hT_lo_ready, 2 * (b * TT + t) + 2)
                tok = slice(t * P, (t + 1) * P)
                n = 0
                for k in range(KT):
                    for g, h in ((gw_hi, hT_hi), (gw_lo, hT_hi), (gw_hi, hT_lo)):
                        last = T.matmul(ps[0:4, 0, tok], g[:, k, :], h[:, k, tok],
                                        start=n == 0, stop=n == 3 * KT - 1)
                        n += 1
                if t == TT - 1:
                    last.then_inc(logitT_ps, 1)

            def gate_turn(b):
                pe.wait_ge(vt_ready, 2 * b + 2)
                T.matmul(ps[:, 1, 0:2 * TT], ones[:], vt[:].rearrange("p a t -> p (a t)"), start=True, stop=True
                         ).then_inc(ratio_ps, 1)
                pe.wait_ge(logitT_ready, b + 1)
                for t in range(TT):
                    last = T.transpose(ps[:, 4, 4 * t:4 * t + 4], lgT[:, t * P:(t + 1) * P], ident[0:4, 0:4])
                last.then_inc(logit_ps, 1)

            pe.wait_ge(const_ready, 7)
            for t in range(TT):
                transpose_q1(t)
            row_sums(0)
            attention(0)
            pe.wait_ge(y_ready, 2 * TT - 2)
            row_sums(1)
            pe.wait_ge(small_in, 16 * SMALL)
            T.transpose(ps[:, 7, 64:64 + NE * KT], b1n[:], ident[0:NE * KT, 0:NE * KT]).then_inc(b1T_ps, 1)
            pe.wait_ge(col_ready, 2)
            for t in range(TT):
                if t == 1:
                    pe.wait_ge(rterm_ready, 2)
                    pe.wait_ge(b1T_ready, 1)
                transpose_h(0, t)
                if t:
                    if t == 1:
                        pe.wait_ge(y_ready, 2 * TT)
                        pe.wait_ge(gw_ready, 1)
                    gate_product(0, t - 1)
            gate_product(0, TT - 1)
            gate_turn(0)
            pe.wait_ge(exp_in, 1)
            attention(1)
            pe.wait_ge(y_ready, 4 * TT)

            with pe.Fori(0, B) as b:
                for s in range(TOP_K):
                    p = b * TOP_K + s
                    for f in range(KT):
                        j, g = f // TT, f % TT
                        if f >= 2:
                            pe.wait_ge(act_ready, p * KT + f - 1)
                        n = 0
                        fs = slice(g * P, (g + 1) * P)
                        for k in range(KT):
                            if g == 0 and k % 2 == 0:
                                pe.wait_ge(raw_done, p * (UNITS * CH) + (CTXN + CH * j + k // 2 + 1))
                            for w, h in ((w_hi, hT_hi), (w_hi, hT_lo), (w_lo, hT_hi)):
                                last = T.matmul(ps[:, f % 2, :], w[j][:, k, fs], h[:, k, :],
                                                start=n == 0, stop=n == 3 * KT - 1)
                                n += 1
                        last.then_inc(g1_done, 1)
                    for m in range(2 * TT):
                        j, t = m // TT, m % TT
                        if m >= 2:
                            pe.wait_ge(y2_done, p * KT + m - 1)
                        n = 0
                        tok = slice(t * P, (t + 1) * P)
                        for k in range(KT):
                            if t == 0 and k % 2 == 0:
                                pe.wait_ge(raw_done, p * (UNITS * CH) + (CTXN + CH * (2 + j) + k // 2 + 1))
                            if m == 0:
                                pe.wait_ge(act_lo_ready, p * KT + k + 1)
                            for a, w in ((act_hi, w_hi), (act_hi, w_lo), (act_lo, w_hi)):
                                last = T.matmul(ps[:, 2 + m % 2, :], a[:, k, tok], w[j][:, k, :],
                                                start=n == 0, stop=n == 3 * KT - 1)
                                n += 1
                        last.then_inc(g2_done, 1)
                        if s == 1 and m < 3:
                            with pe.If(b == 0):
                                if m < 2:
                                    transpose_h(1, 2 * m)
                                    transpose_h(1, 2 * m + 1)
                                if m:
                                    gate_product(1, 2 * m - 2)
                                    gate_product(1, 2 * m - 1)
                                if m == 2:
                                    gate_turn(1)


_INS = ["x", "ctx_4096", "L0_xattn_x1_scale", "L0_xattn_x1_zp", "L0_xattn_x2_scale", "L0_xattn_x2_zp",
        "L0_ffn_gate_w", "L0_ffn_gate_b", "L0_ffn_w1", "L0_ffn_b1", "L0_ffn_w2", "L0_ffn_b2"]


def kernel(**inputs):
    import numpy as np
    import concourse.bacc as bacc
    from concourse.bass_utils import run_bass_kernel_spmd

    nc = bacc.Bacc("TRN2", target_bir_lowering=False, num_devices=1)
    arrays, args = {}, []
    for name in _INS:
        a = np.ascontiguousarray(inputs[name])
        arrays[f"in_{name}_dram"] = a
        args.append(nc.dram_tensor(f"in_{name}_dram", a.shape, mybir.dt.from_np(a.dtype), kind="ExternalInput").ap())
    out = nc.dram_tensor("out_0_dram", (B, S, D), F32, kind="ExternalOutput").ap()
    build(nc, *args, out)
    r = run_bass_kernel_spmd(nc, [arrays], core_ids=[0])
    return r.results[0]["out_0_dram"]
```

```python
from contextlib import ExitStack

import concourse.bass as bass
from concourse import mybir

B, S, D = 2, 512, 1024
KC = 1024
P = 128
NE = 3
TOP_K = 2
VISION = int(S * 0.3)
LN_EPS = 1e-5
QC = 128.0

TT = S // P
KT = D // P
H = D // 2
PAIRS = B * TOP_K
UNITS = 4
CH = 4
RAW = 8
CTXN = B * KT

ALU = mybir.AluOpType
ACT = mybir.ActivationFunctionType
AX = mybir.AxisListType
F32 = mybir.dt.float32
F32R = mybir.dt.float32r
BF16 = mybir.dt.bfloat16
U8 = mybir.dt.uint8
I32 = mybir.dt.int32

ATT_BANK = [[0, 2, 6, 0], [2, 0, 4, 6]]
COL_BANK = [4, 6]
ROW_BANK = [6, 7]
Q1T_BANK = [6, 7, 6, 7, 4, 5, 4, 5]
B1T_BANK = 7
HT_BANK = [[4, 0], [4, 6]]
LOGIT_BANK = [6, 0]
RATIO_BANK = [7, 1]
TURN_BANK = 4

EXPERT_ACT = [ACT.Tanh, ACT.Gelu, ACT.Silu]


def build(nc, x, ctx_in, s1, z1, s2, z2, gate_w, gate_b, w1, b1, w2, b2, out):
    x_v = x.rearrange("b (t p) d -> (b t) p d", p=P)
    out_v = out.rearrange("b (t p) d -> (b t) p d", p=P)
    ctx_v = ctx_in.rearrange("b (k p) n -> (b k) p n", p=P)
    w1_v = w1.rearrange("e (k p) n -> p (e k) n", p=P)
    w2_v = w2.rearrange("e (k p) n -> p (e k) n", p=P)
    b1_v = b1.rearrange("e (f p) -> (e f) p", p=P)

    with ExitStack() as st:
        at = [(nc.sbuf_base + 63) // 64 * 64]

        def sb(name, shape, dt, offset=None):
            size = {F32: 4, F32R: 4, I32: 4, BF16: 2, U8: 1}[dt]
            for n in shape[1:]:
                size *= n
            here = at[0] if offset is None else offset
            if offset is None:
                at[0] += (size + 31) // 32 * 32
            return nc.alloc_sbuf_tensor_at(name, shape, dt, offset=here)

        def sem(name):
            return st.enter_context(nc.semaphore(name))

        w_hi, w_lo = [], []
        w_slot = []
        for i in range(2):
            w_slot.append(at[0])
            w_hi.append(sb(f"w_hi{i}", [P, KT, H], F32R))
            w_lo.append(sb(f"w_lo{i}", [P, KT, H], F32R))
        raw = sb("raw", [P, RAW, D], F32)
        xres = sb("xres", [P, B * TT, D], F32)
        hT_hi = sb("hT_hi", [P, KT, S], F32R)
        hT_lo = sb("hT_lo", [P, KT, S], F32R)
        act_at = at[0]
        act_hi = sb("act_hi", [P, KT, S], F32R)
        act_lo = sb("act_lo", [P, KT, S], F32R)
        hbuf = sb("hbuf", [P, 2, D], F32)
        b2row = hbuf[:, 0, :]
        scratch = sb("scratch", [P, 2, H], F32)
        lgT = [raw[0:8, 1, 0:S], scratch[0:8, 0, :]]
        ctxq = [sb(f"ctxq{b}", [P, KT, D], BF16, act_at + b * KT * D * 2) for b in range(B)]
        o = w_slot[1]
        q1T = []
        for b in range(B):
            q1T.append(sb(f"q1T{b}", [P, KT, S], BF16, o)); o += KT * S * 2
        q1 = sb("q1", [P, 2, D], BF16, o); o += 2 * D * 2
        q1u = sb("q1u", [P, 2, D], U8, o); o += 2 * D
        ctxu = sb("ctxu", [P, 2, D], U8, o); o += 2 * D
        term_cols = sb("term_cols", [P, D], F32R, o); o += D * 4
        term_rows = sb("term_rows", [P, S], F32R, o); o += S * 4

        ident = sb("ident", [P, P], F32)
        ident_b = sb("ident_b", [P, P], BF16)
        ones = sb("ones", [P, P], F32)
        ones_b = sb("ones_b", [P, P], BF16)
        vis_text = sb("vis_text", [P, 2, TT], F32)
        gw = sb("gw", [P, KT, 4], F32)
        gw_parts = sb("gw_parts", [P, KT, 8], F32R)
        gw_last = sb("gw_last", [P, NE], F32)
        gb = sb("gb", [P, NE], F32)
        b1n = sb("b1n", [NE * KT, P], F32)
        b1T = sb("b1T", [P, NE * KT], F32)
        qp = sb("qp", [P, 4], F32)
        qc = sb("qc", [P, 8], F32)
        inv1, inv2, s12, d1, d2, cd, kd = (qc[:, i:i + 1] for i in range(7))
        q1_scale = sb("q1_scale", [P, B * TT], F32)
        q1_bias = sb("q1_bias", [P, B * TT], F32)
        bn = sb("bn", [P, TT, 2, 6], F32)
        mv = sb("mv", [P, TT, 2], F32)
        var = sb("var", [P, TT], F32)
        std = sb("std", [P, TT], F32)
        rt = sb("rt", [P, 3, TT], F32)
        rstd = sb("rstd", [P, TT], F32)
        absum = sb("absum", [P, B * TT], F32)
        vt = sb("vt", [P, 2, TT], F32)
        vts = sb("vts", [P, 2], F32)
        ratio = sb("ratio", [P, 3], F32)
        gbias = sb("gbias", [P, NE], F32)
        lg = sb("lg", [P, NE, TT], F32)
        ex = sb("ex", [P, NE, TT], F32)
        sc = sb("sc", [P, NE, TT], F32)
        sel = sb("sel", [P, 8, TT], F32)
        pick = sb("pick", [1, 8], F32)
        expert = sb("expert", [1, PAIRS], I32)
        gate = sb("gate", [P, PAIRS * TT], F32)

        ps = st.enter_context(nc.psum_tensor("ps", [P, 8, 512], F32))

        x_in = [sem(f"x_in{i}") for i in range(B * TT)]
        raw_in = [sem(f"raw_in{i}") for i in range(RAW)]
        small_in = sem("small_in")
        gw_in = sem("gw_in")
        b2_in = sem("b2_in")
        raw_done = sem("raw_done")
        const_ready = sem("const_ready")
        qc_ready = sem("qc_ready")
        gw_ready = sem("gw_ready")
        rowsum_ps = sem("rowsum_ps")
        logitT_ps = sem("logitT_ps")
        logitT_ready = sem("logitT_ready")
        scales_in = sem("scales_in")
        dve_step = sem("dve_step")
        var_ready = sem("var_ready")
        std_ready = sem("std_ready")
        q1u_ready = sem("q1u_ready")
        q1_ready = sem("q1_ready")
        q1T_ps = sem("q1T_ps")
        q1T_ready = sem("q1T_ready")
        ctxq_ready = sem("ctxq_ready")
        attn_done = sem("attn_done")
        colsum_ps = sem("colsum_ps")
        row_full = sem("row_full")
        col_full = sem("col_full")
        row_term_ready = sem("row_term_ready")
        col_term_ready = sem("col_term_ready")
        q1_scale_ready = sem("q1_scale_ready")
        term_const = sem("term_const")
        term_hi = sem("term_hi")
        x1_ready = sem("x1_ready")
        h_ready = sem("h_ready")
        hT_ps = sem("hT_ps")
        hT_hi_ready = sem("hT_hi_ready")
        hT_lo_ready = sem("hT_lo_ready")
        abs_ready = sem("abs_ready")
        vt_ready = sem("vt_ready")
        ratio_ps = sem("ratio_ps")
        logit_ps = sem("logit_ps")
        exp_in = sem("exp_in")
        exp_ready = sem("exp_ready")
        sel_ready = sem("sel_ready")
        b1T_ps = sem("b1T_ps")
        b1T_ready = sem("b1T_ready")
        w_hi_ready = sem("w_hi_ready")
        g1_done = sem("g1_done")
        act_ready = sem("act_ready")
        act_lo_ready = sem("act_lo_ready")
        g2_done = sem("g2_done")
        y2_done = sem("y2_done")
        b2_used = sem("b2_used")
        out_done = [sem(f"out_done{b}") for b in range(B)]
        SMALL = 3

        def raw_chunk(n):
            return raw[:, n, :].rearrange("p (k n) -> p k n", k=2)

        block = st.enter_context(nc.Block())

        def store_results(eng, b):
            for m in range(2 * TT):
                eng.wait_ge(y2_done, (TOP_K * b + TOP_K - 1) * 2 * TT + m + 1)
                t, c = b * TT + m % TT, (m // TT) * H
                eng.dma_start(out_v[t, :, c:c + H], xres[:, t, c:c + H]).then_inc(out_done[b], 16)
            eng.wait_ge(out_done[b], 16 * 2 * TT)

        @block.sync
        def _(sp):
            def load_x(i):
                sp.dma_start(xres[:, i, :], x_v[i]).then_inc(x_in[i], 16)

            def load_ctx(c):
                if c >= RAW:
                    sp.wait_ge(raw_done, c - RAW + 1)
                sp.dma_start(raw[:, c % RAW, :], ctx_v[c]).then_inc(raw_in[c % RAW], 16)

            load_x(0)
            load_x(1)
            with nc.allow_non_contiguous_dma(reason="small operands"):
                for i, a in enumerate((s1, z1, s2, z2)):
                    sp.dma_start(qp[:, i:i + 1], a.to_broadcast([P, 1])).then_inc(scales_in, 16)
                load_x(2)
                load_x(3)
                for c in range(4):
                    load_ctx(c)
                load_x(4)
                load_x(5)
                sp.dma_start(gw_last[:], gate_w[D:D + 1, :].to_broadcast([P, NE])).then_inc(small_in, 16)
                sp.dma_start(gb[:], gate_b.rearrange("(a e) -> a e", a=1).to_broadcast([P, NE])
                             ).then_inc(small_in, 16)
                sp.dma_start(b1n[:], b1_v).then_inc(small_in, 16)
            for c in range(4, KT):
                load_ctx(c)
            load_x(6)
            load_x(7)
            sp.wait_ge(const_ready, 3)
            with nc.allow_non_contiguous_dma(reason="small operands"):
                sp.dma_start(gw[:, :, 0:NE], gate_w[0:D, :].rearrange("(k p) e -> p k e", p=P)
                             ).then_inc(gw_in, 16)
            for c in range(KT, CTXN):
                load_ctx(c)
            with sp.Fori(0, PAIRS) as p:
                sp.wait_ge(sel_ready, p + 1)
                e = sp.value_load(expert[0:1, bass.ds(p, 1)], min_val=0, max_val=NE - 1)
                for j in range(UNITS):
                    w_v = w1_v if j < 2 else w2_v
                    for g in range(CH):
                        n = CH * j + g
                        sp.wait_ge(raw_done, p * (UNITS * CH) + (CTXN + n - RAW + 1))
                        sp.dma_start(raw_chunk(n % RAW),
                                     w_v[:, bass.ds(e * KT + 2 * g, 2), (j % 2) * H:(j % 2 + 1) * H],
                                     ).then_inc(raw_in[n % RAW], 16)
                        if n == RAW:
                            sp.dma_start(b2row, b2[bass.ds(e, 1), :].to_broadcast([P, D])).then_inc(b2_in, 16)

            store_results(sp, 1)

        @block.gpsimd
        def _(pool):
            nc.gpsimd.memset(ones[:], 1.0).then_inc(const_ready, 1)
            nc.gpsimd.memset(ones_b[:], 1.0).then_inc(const_ready, 1)
            nc.gpsimd.memset(gw[:], 0.0).then_inc(const_ready, 1)
            pool.wait_ge(const_ready, 3)
            nc.gpsimd.affine_select(out=ident[:], in_=ones[:], compare_op=ALU.is_equal, fill=0.0, base=0,
                                    pattern=[[-1, P]], channel_multiplier=1).then_inc(const_ready, 1)
            nc.gpsimd.affine_select(out=ident_b[:], in_=ones_b[:], compare_op=ALU.is_equal, fill=0.0, base=0,
                                    pattern=[[-1, P]], channel_multiplier=1).then_inc(const_ready, 1)
            nc.gpsimd.affine_select(out=vis_text[:, 0, :], in_=ones[:, 0:TT], compare_op=ALU.is_ge, fill=0.0,
                                    base=VISION - 1, pattern=[[-P, TT]], channel_multiplier=-1
                                    ).then_inc(const_ready, 1)
            nc.gpsimd.affine_select(out=vis_text[:, 1, :], in_=ones[:, 0:TT], compare_op=ALU.is_ge, fill=0.0,
                                    base=-VISION, pattern=[[P, TT]], channel_multiplier=1
                                    ).then_inc(const_ready, 1)

            nc.gpsimd.memset(term_cols[:].bitcast(F32), 0.0).then_inc(term_const, 1)
            nc.gpsimd.memset(term_rows[:].bitcast(F32), 0.0).then_inc(term_const, 1)
            pool.wait_ge(term_const, 2)
            for i in (0, 32):
                nc.gpsimd.memset(term_rows[i:i + 1, :].bitcast(F32), 1.0).then_inc(term_const, 1)
                nc.gpsimd.memset(term_cols[64 + i:65 + i, :].bitcast(F32), 1.0).then_inc(term_const, 1)
            pool.wait_ge(term_const, 6)

            def centre_ctx(c):
                pool.wait_ge(raw_done, c + 1)
                nc.gpsimd.tensor_scalar(ctxq[c // KT][:, c % KT, :], ctxu[:, c % 2, :], -QC, 1.0,
                                        ALU.add, ALU.mult).then_inc(ctxq_ready, 1)

            def centre_q1(i):
                pool.wait_ge(q1u_ready, i + 1)
                if i >= 2:
                    pool.wait_ge(q1T_ps, i - 1)
                nc.gpsimd.tensor_scalar(q1[:, i % 2, :], q1u[:, i % 2, :], -QC, 1.0,
                                        ALU.add, ALU.mult).then_inc(q1_ready, 1)

            centre_q1(0)
            centre_q1(1)
            for k in range(4):
                centre_ctx(k)
            centre_q1(2)
            centre_q1(3)
            for k in range(4, CTXN):
                centre_ctx(k)
                if k in (6, 7):
                    centre_q1(k - 2)
                if k in (KT + 4, KT + 5):
                    centre_q1(k - KT + 2)
            pool.wait_ge(ctxq_ready, B * KT)
            pool.wait_ge(attn_done, TT)
            full = scratch[:].rearrange("p a n -> p (a n)")
            pool.wait_ge(col_full, 4)
            nc.gpsimd.tensor_copy(term_cols[0:33, :], full[0:33]).then_inc(term_hi, 1)
            pool.wait_ge(term_hi, 1)
            nc.gpsimd.tensor_tensor(term_cols[32:33, :], full[32:33], term_cols[32:33, :].bitcast(F32),
                                    ALU.subtract).then_inc(col_term_ready, 1)
            pool.wait_ge(col_term_ready, 2)
            pool.wait_ge(row_full, 2)
            nc.gpsimd.tensor_copy(term_rows[64:97, :], scratch[64:97, 0, :]).then_inc(term_hi, 1)
            pool.wait_ge(term_hi, 2)
            nc.gpsimd.tensor_tensor(term_rows[96:97, :], scratch[96:97, 0, :], term_rows[96:97, :].bitcast(F32),
                                    ALU.subtract).then_inc(row_term_ready, 1)
            store_results(pool, 0)

        @block.scalar
        def _(act):
            def sqrt_var(i, a, z):
                act.wait_ge(var_ready, i)
                nc.scalar.activation(std[:, a:z], var[:, a:z], ACT.Sqrt).then_inc(std_ready, 1)

            def quant_ctx(c):
                act.wait_ge(raw_in[c % RAW], 16 * (c // RAW + 1))
                if c >= 2:
                    act.wait_ge(ctxq_ready, c - 1)
                nc.scalar.activation(ctxu[:, c % 2, :], raw[:, c % RAW, :], ACT.Identity,
                                     bias=qp[:, 3:4], scale=inv2).then_inc(raw_done, 1)

            def quant_x(i):
                act.wait_ge(q1_scale_ready, i // 2 + 1)
                if i >= 2:
                    act.wait_ge(q1_ready, i - 1)
                nc.scalar.activation(q1u[:, i % 2, :], xres[:, i, :], ACT.Identity,
                                     bias=q1_bias[:, i:i + 1], scale=q1_scale[:, i:i + 1]).then_inc(q1u_ready, 1)

            def full_row_term(b):
                act.wait_ge(rowsum_ps, b + 1)
                if b:
                    act.wait_ge(row_term_ready, b)
                nc.scalar.activation(scratch[64:97, 0, :], ps[64:97, ROW_BANK[b], :], ACT.Identity,
                                     bias=cd[64:97], scale=d2[64:97]).then_inc(row_full, 1)

            def full_col_term(b):
                act.wait_ge(colsum_ps, b + 1)
                if b:
                    act.wait_ge(col_term_ready, b)
                for c in range(2):
                    nc.scalar.activation(scratch[0:33, c, :], ps[0:33, COL_BANK[b] + c, :], ACT.Copy,
                                         scale=d1[0:33]).then_inc(col_full, 1)

            def sum_h(b, t):
                i = b * TT + t
                act.wait_ge(h_ready, i + 1)
                if i:
                    act.wait_ge(abs_ready, i)
                junk = scratch[:].rearrange("p a n -> p (a n)") if b else raw[:, 0, :]
                nc.scalar.activation(junk, hbuf[:, t % 2, :], ACT.Abs,
                                     accum_out=absum[:, i:i + 1]).then_inc(abs_ready, 1)

            def split_h(b, t):
                i = b * TT + t
                act.wait_ge(hT_ps, i + 1)
                for c in range(2):
                    nc.scalar.activation(hT_hi[:, 4 * c:4 * c + 4, t * P:(t + 1) * P],
                                         ps[:, HT_BANK[b][t % 2] + c, :].rearrange("p (k s) -> p k s", k=4),
                                         ACT.Copy).then_inc(hT_hi_ready, 1)

            def gate_logits(b):
                act.wait_ge(logitT_ps, b + 1)
                nc.scalar.activation(lgT[b], ps[0:8, LOGIT_BANK[b], :], ACT.Copy).then_inc(logitT_ready, 1)

            def gate_exp(b):
                act.wait_ge(exp_in, b + 1)
                nc.scalar.activation(ex[:], lg[:], ACT.Exp).then_inc(exp_ready, 1)

            def load_q1T(t):
                act.wait_ge(q1T_ps, TT + t + 1)
                nc.scalar.activation(q1T[1][:, :, t * P:(t + 1) * P],
                                     ps[:, Q1T_BANK[TT + t], :].bitcast(BF16).rearrange("p (k s) -> p k s", k=KT),
                                     ACT.Copy).then_inc(q1T_ready, 1)

            nc.scalar.preload_act_table(ACT.Sqrt)
            sqrt_var(1, 0, 2)
            quant_x(0)
            quant_x(1)
            quant_ctx(0)
            sqrt_var(2, 2, 4)
            for k in range(1, 4):
                quant_ctx(k)
            quant_x(2)
            quant_x(3)
            quant_ctx(4)
            sqrt_var(3, 0, 2)
            quant_ctx(5)
            quant_ctx(6)
            quant_x(4)
            quant_ctx(7)
            quant_x(5)
            act.wait_ge(b1T_ps, 1)
            nc.scalar.activation(b1T[:], ps[:, B1T_BANK, 0:NE * KT], ACT.Copy).then_inc(b1T_ready, 1)
            full_row_term(0)
            full_col_term(0)
            quant_ctx(8)
            sqrt_var(4, 2, 4)
            for c in range(9, 13):
                quant_ctx(c)
            load_q1T(0)
            load_q1T(1)
            quant_x(6)
            quant_ctx(13)
            quant_x(7)
            quant_ctx(14)
            load_q1T(2)
            sqrt_var(5, 0, 2)
            quant_ctx(15)
            load_q1T(3)
            sum_h(0, 0)
            split_h(0, 0)
            sum_h(0, 1)
            full_col_term(1)
            sqrt_var(6, 2, 4)
            split_h(0, 1)
            full_row_term(1)
            sum_h(0, 2)
            split_h(0, 2)
            sum_h(0, 3)
            split_h(0, 3)
            nc.scalar.preload_act_table(ACT.Exp)
            gate_logits(0)
            gate_exp(0)

            def w_hi_chunk(freed, p, n):
                u, g = n // CH, n % CH
                act.wait_ge(raw_in[n % RAW], p * (16 * UNITS * CH // RAW) + 16 * (CTXN // RAW + n // RAW + 1))
                if g == 0 and freed is not None:
                    act.wait_ge(*freed)
                nc.scalar.activation(w_hi[u % 2][:, 2 * g:2 * g + 2, :], raw_chunk(n % RAW), ACT.Copy
                                     ).then_inc(w_hi_ready, 1)

            for g in range(CH):
                w_hi_chunk(None, 0, g)

            act.wait_ge(b1T_ready, 1)
            with act.Fori(0, B) as b:
                for s in range(TOP_K):
                    p = b * TOP_K + s
                    if s == 1:
                        with act.If(b == 0):
                            sqrt_var(7, 0, TT)
                    e = act.value_load(expert[0:1, bass.ds(p, 1)], min_val=0, max_val=NE - 1)
                    for ee in range(NE):
                        with act.If(e == ee):
                            nc.scalar.preload_act_table(EXPERT_ACT[ee])
                            for f in range(KT):
                                j, g = f // TT, f % TT
                                act.wait_ge(g1_done, p * KT + f + 1)
                                if f >= 2:
                                    act.wait_ge(act_lo_ready, p * KT + f - 1)
                                bias = b1T[:, ee * KT + f:ee * KT + f + 1]
                                nc.scalar.activation(scratch[:, f % 2, :], ps[:, f % 2, :], EXPERT_ACT[ee],
                                                     bias=bias)
                                nc.scalar.activation(act_hi[:, f, :], ps[:, f % 2, :], EXPERT_ACT[ee],
                                                     bias=bias).then_inc(act_ready, 1)
                                w_hi_chunk((g1_done, p * KT + (TT if j else 1)), p, CH * (j + 1) + g)
                    for g in range(CH):
                        w_hi_chunk((g1_done, p * KT + 2 * TT), p, CH * 3 + g)
                    if s == 0:
                        for g in range(CH):
                            w_hi_chunk((g2_done, p * KT + TT), p, CH * 4 + g)
                    else:
                        with act.If(b == 0):
                            for t in range(TT):
                                sum_h(1, t)
                                split_h(1, t)
                            gate_logits(1)
                            gate_exp(1)
                            for g in range(CH):
                                w_hi_chunk((g2_done, 2 * KT - TT), 1, CH * 4 + g)

        @block.vector
        def _(dve):
            steps = [0]

            def then(ins):
                steps[0] += 1
                ins.then_inc(dve_step, 1)
                dve.wait_ge(dve_step, steps[0])

            V = nc.vector

            def tile_stats(b, t, src):
                for c in range(2):
                    last = V.bn_stats(bn[:, t, c, :], src[:, c * H:(c + 1) * H])
                then(last)
                then(V.bn_aggr(mv[:, t, :], bn[:, t].rearrange("p a s -> p (a s)")))

            def var_out(a, z):
                V.tensor_scalar(var[:, a:z], mv[:, a:z, 1], LN_EPS, None, ALU.add).then_inc(var_ready, 1)

            def rsqrt(i, a, z):
                r0, r1, r2 = (rt[:, j, a:z] for j in range(3))
                dve.wait_ge(std_ready, i)
                then(V.reciprocal(r0, std[:, a:z]))
                then(V.tensor_tensor(r1, r0, var[:, a:z], ALU.mult))
                then(V.tensor_tensor(r2, r1, r0, ALU.mult))
                then(V.tensor_scalar(r1, r2, -0.5, 1.5, ALU.mult, ALU.add))
                then(V.tensor_tensor(rstd[:, a:z], r1, r0, ALU.mult))

            def q1_scales(b, a, z):
                scale, bias = q1_scale[:, b * TT + a:b * TT + z], q1_bias[:, b * TT + a:b * TT + z]
                then(V.tensor_scalar(scale, rstd[:, a:z], inv1, None, ALU.mult))
                then(V.tensor_tensor(bias, scale, mv[:, a:z, 0], ALU.mult))
                V.tensor_scalar(bias, bias, -1.0, qp[:, 1:2], ALU.mult, ALU.add).then_inc(q1_scale_ready, 1)

            def x_stats(b, t):
                dve.wait_ge(x_in[b * TT + t], 16)
                tile_stats(b, t, xres[:, b * TT + t, :])

            def load_q1T(t):
                dve.wait_ge(q1T_ps, t + 1)
                V.tensor_copy(q1T[0][:, :, t * P:(t + 1) * P],
                              ps[:, Q1T_BANK[t], :].bitcast(BF16).rearrange("p (k s) -> p k s", k=KT)
                              ).then_inc(q1T_ready, 1)

            def split_row_term():
                dve.wait_ge(term_const, 6)
                dve.wait_ge(row_full, 1)
                then(V.tensor_copy(term_rows[64:97, :], scratch[64:97, 0, :]))
                V.tensor_tensor(term_rows[96:97, :], scratch[96:97, 0, :], term_rows[96:97, :].bitcast(F32),
                                ALU.subtract).then_inc(row_term_ready, 1)

            def split_col_term():
                full = scratch[:].rearrange("p a n -> p (a n)")
                dve.wait_ge(col_full, 2)
                then(V.tensor_copy(term_cols[0:33, :], full[0:33]))
                V.tensor_tensor(term_cols[32:33, :], full[32:33], term_cols[32:33, :].bitcast(F32),
                                ALU.subtract).then_inc(col_term_ready, 1)

            def attn_add(b, t):
                i = b * TT + t
                dve.wait_ge(attn_done, i + 1)
                for c in range(2):
                    xt = xres[:, i, c * H:(c + 1) * H]
                    last = V.scalar_tensor_tensor(out=xt, in0=ps[:, ATT_BANK[b][t] + c, :], scalar=s12, in1=xt,
                                                  op0=ALU.mult, op1=ALU.add)
                last.then_inc(x1_ready, 1)

            def x1_stats(b, t):
                i = b * TT + t
                dve.wait_ge(x1_ready, i + 1)
                tile_stats(b, t, xres[:, i, :])

            def h_tile(b, t):
                i = b * TT + t
                if b and t == 0:
                    dve.wait_ge(b2_used, TOP_K * TT)
                if t >= 2:
                    dve.wait_ge(hT_ps, i - 1)
                    dve.wait_ge(abs_ready, i - 1)
                V.tensor_scalar(hbuf[:, t % 2, :], xres[:, i, :], mv[:, t, 0:1], rstd[:, t:t + 1],
                                ALU.subtract, ALU.mult).then_inc(h_ready, 1)

            def h_lo(b, t):
                i = b * TT + t
                for c in range(2):
                    dve.wait_ge(hT_hi_ready, 2 * i + c + 1)
                    V.tensor_tensor(hT_lo[:, 4 * c:4 * c + 4, t * P:(t + 1) * P],
                                    ps[:, HT_BANK[b][t % 2] + c, :].rearrange("p (k s) -> p k s", k=4),
                                    hT_hi[:, 4 * c:4 * c + 4, t * P:(t + 1) * P].bitcast(F32),
                                    ALU.subtract).then_inc(hT_lo_ready, 1)

            def tokens_abs(b):
                dve.wait_ge(abs_ready, (b + 1) * TT)
                ab = absum[:, b * TT:(b + 1) * TT]
                V.tensor_tensor(vt[:, 0, :], vis_text[:, 0, :], ab, ALU.mult).then_inc(vt_ready, 1)
                V.tensor_tensor(vt[:, 1, :], vis_text[:, 1, :], ab, ALU.mult).then_inc(vt_ready, 1)

            def router_bias(b):
                dve.wait_ge(ratio_ps, b + 1)
                if b == 0:
                    dve.wait_ge(small_in, 16 * SMALL)
                then(V.tensor_reduce(vts[:], ps[:, RATIO_BANK[b], 0:2 * TT].rearrange("p (a t) -> p a t", a=2),
                                     AX.X, ALU.add))
                then(V.tensor_scalar(ratio[:, 0:1], vts[:, 0:1], 1.0 / (VISION * D), 1e-8, ALU.mult, ALU.add))
                then(V.reciprocal(ratio[:, 1:2], ratio[:, 0:1]))
                then(V.tensor_scalar(ratio[:, 2:3], vts[:, 1:2], 1.0 / ((S - VISION) * D), ratio[:, 1:2],
                                     ALU.mult, ALU.mult))
                then(V.scalar_tensor_tensor(out=gbias[:], in0=gw_last[:], scalar=ratio[:, 2:3], in1=gb[:],
                                            op0=ALU.mult, op1=ALU.add))

            def choose(b):
                dve.wait_ge(logit_ps, b + 1)
                lps = ps[:, TURN_BANK, 0:8 * TT].rearrange("p (t e) -> p e t", e=8)
                for e in range(NE):
                    last = V.tensor_scalar(sc[:, e, :], lps[:, e, :], gbias[:, e:e + 1], None, ALU.add)
                then(last)
                for e in range(NE):
                    last = V.tensor_tensor(sc[:, e, :], lps[:, 4 + e, :], sc[:, e, :], ALU.add)
                then(last)
                top, low, mid, a, c = (sel[:, i, :] for i in range(5))
                then(V.tensor_tensor(a, sc[:, 0, :], sc[:, 1, :], ALU.max))
                then(V.tensor_tensor(top, a, sc[:, 2, :], ALU.max))
                for e in range(NE):
                    last = V.tensor_tensor(lg[:, e, :], sc[:, e, :], top, ALU.subtract)
                last.then_inc(exp_in, 1)
                dve.wait_ge(exp_ready, b + 1)
                V.tensor_tensor(a, ex[:, 0, :], ex[:, 1, :], ALU.max)
                then(V.tensor_tensor(c, ex[:, 0, :], ex[:, 1, :], ALU.min))
                V.tensor_tensor(low, c, ex[:, 2, :], ALU.min)
                then(V.tensor_tensor(top, a, ex[:, 2, :], ALU.max))
                one = lambda i: pick[0:1, i:i + 1]
                e0 = lambda e: ex[0:1, e, 0:1]
                V.tensor_tensor(one(0), e0(0), top[0:1, 0:1], ALU.is_lt)
                V.tensor_tensor(one(1), e0(1), top[0:1, 0:1], ALU.is_lt)
                V.tensor_tensor(one(2), e0(1), low[0:1, 0:1], ALU.is_le)
                then(V.tensor_tensor(one(3), e0(2), low[0:1, 0:1], ALU.is_le))
                V.scalar_tensor_tensor(out=expert[0:1, 2 * b:2 * b + 1], in0=one(1), scalar=1.0, in1=one(0),
                                       op0=ALU.add, op1=ALU.mult).then_inc(sel_ready, 1)
                V.scalar_tensor_tensor(out=one(4), in0=one(1), scalar=1.0, in1=one(0),
                                       op0=ALU.add, op1=ALU.mult)
                then(V.scalar_tensor_tensor(out=one(5), in0=one(3), scalar=2.0, in1=one(2),
                                            op0=ALU.mult, op1=ALU.max))
                then(V.tensor_tensor(one(6), one(4), one(5), ALU.add))
                V.tensor_scalar(expert[0:1, 2 * b + 1:2 * b + 2], one(6), -1.0, 3.0, ALU.mult, ALU.add
                                ).then_inc(sel_ready, 1)

            def gate_values(b):
                top, _, mid, a, c, d, e, f = (sel[:, i, :] for i in range(8))
                V.tensor_tensor(mid, a, ex[:, 2, :], ALU.min)
                then(V.tensor_tensor(d, ex[:, 0, :], ex[:, 1, :], ALU.add))
                then(V.tensor_tensor(e, d, ex[:, 2, :], ALU.add))
                V.tensor_tensor(mid, mid, c, ALU.max)
                then(V.reciprocal(f, e))
                V.tensor_tensor(top, top, f, ALU.mult)
                then(V.tensor_tensor(mid, mid, f, ALU.mult))
                then(V.tensor_tensor(a, top, mid, ALU.add))
                then(V.tensor_scalar(c, a, 1e-8, None, ALU.add))
                then(V.reciprocal(a, c))
                V.tensor_tensor(gate[:, 8 * b:8 * b + 4], top, a, ALU.mult)
                then(V.tensor_tensor(gate[:, 8 * b + 4:8 * b + 8], mid, a, ALU.mult))

            def w_lo_chunk(p, n):
                u, g = n // CH, n % CH
                dve.wait_ge(w_hi_ready, p * (UNITS * CH) + n + 1)
                V.tensor_tensor(w_lo[u % 2][:, 2 * g:2 * g + 2, :], raw_chunk(n % RAW),
                                w_hi[u % 2][:, 2 * g:2 * g + 2, :].bitcast(F32), ALU.subtract
                                ).then_inc(raw_done, 1)

            def dve_constants():
                dve.wait_ge(scales_in, 16 * 4)
                V.reciprocal(inv1, qp[:, 0:1])
                V.reciprocal(inv2, qp[:, 2:3])
                V.tensor_tensor(s12, qp[:, 0:1], qp[:, 2:3], ALU.mult)
                V.tensor_scalar(d1, qp[:, 1:2], -1.0, QC, ALU.mult, ALU.add)
                then(V.tensor_scalar(d2, qp[:, 3:4], -1.0, QC, ALU.mult, ALU.add))
                then(V.tensor_scalar(kd, d1, float(KC), None, ALU.mult))
                V.tensor_tensor(cd, kd, d2, ALU.mult).then_inc(qc_ready, 1)

            def gate_weights():
                dve.wait_ge(gw_in, 16)
                then(V.tensor_copy(gw_parts[:, :, 0:4], gw[:]))
                V.tensor_tensor(gw_parts[:, :, 4:8], gw[:], gw_parts[:, :, 0:4].bitcast(F32), ALU.subtract
                                ).then_inc(gw_ready, 1)

            x_stats(0, 0)
            x_stats(0, 1)
            var_out(0, 2)
            dve_constants()
            rsqrt(1, 0, 2)
            q1_scales(0, 0, 2)
            x_stats(0, 2)
            x_stats(0, 3)
            var_out(2, 4)
            load_q1T(0)
            load_q1T(1)
            rsqrt(2, 2, 4)
            q1_scales(0, 2, 4)
            x_stats(1, 0)
            x_stats(1, 1)
            var_out(0, 2)
            rsqrt(3, 0, 2)
            q1_scales(1, 0, 2)
            load_q1T(2)
            load_q1T(3)
            x_stats(1, 2)
            x_stats(1, 3)
            var_out(2, 4)
            split_row_term()
            split_col_term()
            gate_weights()
            attn_add(0, 0)
            rsqrt(4, 2, 4)
            q1_scales(1, 2, 4)
            attn_add(0, 1)
            attn_add(0, 2)
            x1_stats(0, 0)
            x1_stats(0, 1)
            var_out(0, 2)
            attn_add(0, 3)
            rsqrt(5, 0, 2)
            h_tile(0, 0)
            h_tile(0, 1)
            x1_stats(0, 2)
            x1_stats(0, 3)
            var_out(2, 4)
            h_lo(0, 0)
            rsqrt(6, 2, 4)
            h_tile(0, 2)
            h_lo(0, 1)
            h_tile(0, 3)
            h_lo(0, 2)
            tokens_abs(0)
            h_lo(0, 3)
            router_bias(0)
            choose(0)
            gate_values(0)
            attn_add(1, 0)
            attn_add(1, 1)
            for g in range(CH):
                w_lo_chunk(0, g)
            x1_stats(1, 0)
            x1_stats(1, 1)
            attn_add(1, 2)
            x1_stats(1, 2)
            attn_add(1, 3)
            x1_stats(1, 3)
            var_out(0, TT)

            with dve.Fori(0, B) as b:
                for s in range(TOP_K):
                    p = b * TOP_K + s
                    if s == 1:
                        with dve.If(b == 0):
                            rsqrt(7, 0, TT)
                    for f in range(KT):
                        dve.wait_ge(act_ready, p * KT + f + 1)
                        V.tensor_tensor(act_lo[:, f, :], scratch[:, f % 2, :], act_hi[:, f, :].bitcast(F32),
                                        ALU.subtract).then_inc(act_lo_ready, 1)
                        w_lo_chunk(p, CH * (f // TT + 1) + f % TT)
                        if f >= TT:
                            t = f - TT
                            if t == 0:
                                dve.wait_ge(b2_in, p * 16 + 16)
                                dve.wait_ge(act_lo_ready, p * KT + f)
                            xt = xres[:, bass.ds(b * TT + t, 1), :].rearrange("p a n -> p (a n)")
                            V.scalar_tensor_tensor(out=xt, in0=b2row, scalar=gate[:, bass.ds(p * TT + t, 1)],
                                                   in1=xt, op0=ALU.mult, op1=ALU.add).then_inc(b2_used, 1)

                    def result(m):
                        if m == 0:
                            dve.wait_ge(b2_used, p * TT + TT)
                        dve.wait_ge(g2_done, p * KT + m + 1)
                        c = (m // TT) * H
                        xt = xres[:, bass.ds(b * TT + m % TT, 1), c:c + H].rearrange("p a n -> p (a n)")
                        V.scalar_tensor_tensor(out=xt, in0=ps[:, 2 + m % 2, :],
                                               scalar=gate[:, bass.ds(p * TT + m % TT, 1)],
                                               in1=xt, op0=ALU.mult, op1=ALU.add).then_inc(y2_done, 1)

                    if s == 0:
                        for m in range(TT):
                            w_lo_chunk(p, CH * 3 + m)
                            result(m)
                        for g in range(CH):
                            w_lo_chunk(p, CH * 4 + g)
                            result(TT + g)
                    else:
                        with dve.If(b == 0):
                            h_tile(1, 0)
                            h_tile(1, 1)
                        w_lo_chunk(p, CH * 3)
                        result(0)
                        w_lo_chunk(p, CH * 3 + 1)
                        result(1)
                        with dve.If(b == 0):
                            h_tile(1, 2)
                            h_lo(1, 0)
                            h_tile(1, 3)
                            h_lo(1, 1)
                        w_lo_chunk(p, CH * 3 + 2)
                        w_lo_chunk(p, CH * 3 + 3)
                        result(2)
                        with dve.If(b == 0):
                            tokens_abs(1)
                            h_lo(1, 2)
                            h_lo(1, 3)
                        result(3)
                        with dve.If(b == 0):
                            router_bias(1)
                        result(4)
                        with dve.If(b == 0):
                            choose(1)
                            gate_values(1)
                        result(5)
                        with dve.If(b == 0):
                            w_lo_chunk(1, CH * 4)
                        result(6)
                        with dve.If(b == 0):
                            for g in range(1, CH):
                                w_lo_chunk(1, CH * 4 + g)
                        result(7)

        @block.tensor
        def _(pe):
            T = nc.tensor

            def transpose_q1(i):
                pe.wait_ge(q1_ready, i + 1)
                if i < TT:
                    if i >= 2:
                        pe.wait_ge(q1T_ready, i - 1)
                elif i < TT + 2:
                    pe.wait_ge(col_full, 2)
                else:
                    pe.wait_ge(q1T_ready, i - 1)
                bank = ps[:, Q1T_BANK[i], :].bitcast(BF16)
                for k in range(KT):
                    last = T.transpose(bank[:, k * P:(k + 1) * P], q1[:, i % 2, k * P:(k + 1) * P], ident_b[:])
                last.then_inc(q1T_ps, 1)

            def row_sums(b):
                pe.wait_ge(q1T_ready, b * TT + TT)
                for k in range(KT):
                    last = T.matmul(ps[:, ROW_BANK[b], :], ones_b[:], q1T[b][:, k, :],
                                    start=k == 0, stop=k == KT - 1)
                last.then_inc(rowsum_ps, 1)

            def column_sums(b, k):
                pe.wait_ge(ctxq_ready, b * KT + k + 1)
                for c in range(2):
                    last = T.matmul(ps[:, COL_BANK[b] + c, :], ones_b[:], ctxq[b][:, k, c * H:(c + 1) * H],
                                    start=k == 0, stop=k == KT - 1)
                if k == KT - 1:
                    last.then_inc(colsum_ps, 1)

            def codes_product(b, t, k, halves=(0, 1)):
                for c in halves:
                    T.matmul(ps[:, ATT_BANK[b][t] + c, :], q1T[b][:, k, t * P:(t + 1) * P],
                             ctxq[b][:, k, c * H:(c + 1) * H], start=k == 0, stop=False)

            def add_terms(b, t):
                pe.wait_ge(row_term_ready, b + 1)
                pe.wait_ge(col_term_ready, b + 1)
                for c in range(2):
                    last = T.matmul(ps[:, ATT_BANK[b][t] + c, :], term_rows[:, t * P:(t + 1) * P],
                                    term_cols[:, c * H:(c + 1) * H], start=False, stop=True)
                last.then_inc(attn_done, 1)

            def transpose_h(b, t):
                i = b * TT + t
                pe.wait_ge(h_ready, i + 1)
                if t >= 2:
                    pe.wait_ge(hT_lo_ready, 2 * (i - 1))
                for k in range(KT):
                    last = T.transpose(ps[:, HT_BANK[b][t % 2] + k // 4, (k % 4) * P:(k % 4 + 1) * P],
                                       hbuf[:, t % 2, k * P:(k + 1) * P], ident[:])
                last.then_inc(hT_ps, 1)

            def gate_product(b, t):
                pe.wait_ge(hT_lo_ready, 2 * (b * TT + t) + 2)
                tok = slice(t * P, (t + 1) * P)
                n = 0
                for k in range(KT):
                    for h in (hT_hi, hT_lo):
                        last = T.matmul(ps[0:8, LOGIT_BANK[b], tok], gw_parts[:, k, :], h[:, k, tok],
                                        start=n == 0, stop=n == 2 * KT - 1)
                        n += 1
                if t == TT - 1:
                    last.then_inc(logitT_ps, 1)

            def sum_abs(b):
                pe.wait_ge(vt_ready, 2 * b + 2)
                T.matmul(ps[:, RATIO_BANK[b], 0:2 * TT], ones[:], vt[:].rearrange("p a t -> p (a t)"),
                         start=True, stop=True).then_inc(ratio_ps, 1)

            def gate_turn(b):
                pe.wait_ge(logitT_ready, b + 1)
                for t in range(TT):
                    last = T.transpose(ps[:, TURN_BANK, 8 * t:8 * t + 8], lgT[b][:, t * P:(t + 1) * P], ident[0:8, 0:8])
                last.then_inc(logit_ps, 1)

            pe.wait_ge(const_ready, 7)
            transpose_q1(0)
            transpose_q1(1)
            for k in range(KT):
                column_sums(0, k)
                if k < 2:
                    pe.wait_ge(q1T_ready, 2)
                codes_product(0, 0, k)
                codes_product(0, 1, k)
                if k in (3, 4):
                    transpose_q1(k - 1)
                if k == 6:
                    pe.wait_ge(q1T_ready, TT)
                    pe.wait_ge(small_in, 16 * SMALL)
                    T.transpose(ps[:, B1T_BANK, 0:NE * KT], b1n[:], ident[0:NE * KT, 0:NE * KT]
                                ).then_inc(b1T_ps, 1)
                    row_sums(0)
            pe.wait_ge(b1T_ready, 1)
            for k in range(KT):
                codes_product(0, 2, k, (1,))
            pe.wait_ge(row_full, 1)
            for k in range(KT):
                codes_product(0, 2, k, (0,))
            for t in range(3):
                add_terms(0, t)
            transpose_q1(4)
            transpose_q1(5)
            pe.wait_ge(x1_ready, 1)
            for k in range(KT):
                codes_product(0, 3, k)
            add_terms(0, 3)
            transpose_q1(6)
            pe.wait_ge(x1_ready, 3)
            for k in range(5):
                column_sums(1, k)
            transpose_q1(7)
            for k in range(5):
                codes_product(1, 0, k)
            pe.wait_ge(q1T_ready, 2 * TT)
            transpose_h(0, 0)
            pe.wait_ge(x1_ready, 4)
            transpose_h(0, 1)
            for k in range(5, KT):
                column_sums(1, k)
            for k in range(5, KT):
                codes_product(1, 0, k)
            pe.wait_ge(col_full, 4)
            row_sums(1)
            transpose_h(0, 2)
            pe.wait_ge(gw_ready, 1)
            gate_product(0, 0)
            transpose_h(0, 3)
            gate_product(0, 1)
            gate_product(0, 2)
            pe.wait_ge(row_full, 2)
            sum_abs(0)
            gate_product(0, 3)
            for k in range(2):
                codes_product(1, 1, k)
            gate_turn(0)
            for k in range(2, KT):
                codes_product(1, 1, k)
            add_terms(1, 0)
            add_terms(1, 1)
            pe.wait_ge(exp_in, 1)
            for t in range(2, TT):
                for k in range(KT):
                    codes_product(1, t, k)
                add_terms(1, t)
            pe.wait_ge(x1_ready, TT + 2)

            with pe.Fori(0, B) as b:
                for s in range(TOP_K):
                    p = b * TOP_K + s
                    for f in range(KT):
                        j, g = f // TT, f % TT
                        if f >= 2:
                            pe.wait_ge(act_ready, p * KT + f - 1)
                        n = 0
                        fs = slice(g * P, (g + 1) * P)
                        for k in range(KT):
                            if g == 0 and k % 2 == 0:
                                pe.wait_ge(raw_done, p * (UNITS * CH) + (CTXN + CH * j + k // 2 + 1))
                            for w, h in ((w_hi, hT_hi), (w_hi, hT_lo), (w_lo, hT_hi)):
                                last = T.matmul(ps[:, f % 2, :], w[j][:, k, fs], h[:, k, :],
                                                start=n == 0, stop=n == 3 * KT - 1)
                                n += 1
                        last.then_inc(g1_done, 1)
                    for m in range(2 * TT):
                        j, t = m // TT, m % TT
                        if m >= 2:
                            pe.wait_ge(y2_done, p * KT + m - 1)
                        n = 0
                        tok = slice(t * P, (t + 1) * P)
                        for k in range(KT):
                            if t == 0 and k % 2 == 0:
                                pe.wait_ge(raw_done, p * (UNITS * CH) + (CTXN + CH * (2 + j) + k // 2 + 1))
                            if m == 0:
                                pe.wait_ge(act_lo_ready, p * KT + k + 1)
                            for a, w in ((act_hi, w_hi), (act_hi, w_lo), (act_lo, w_hi)):
                                last = T.matmul(ps[:, 2 + m % 2, :], a[:, k, tok], w[j][:, k, :],
                                                start=n == 0, stop=n == 3 * KT - 1)
                                n += 1
                        last.then_inc(g2_done, 1)
                        if s == 1 and 1 <= m <= 4:
                            with pe.If(b == 0):
                                if m < 3:
                                    transpose_h(1, 2 * m - 2)
                                    transpose_h(1, 2 * m - 1)
                                if m in (2, 3):
                                    gate_product(1, 2 * m - 4)
                                    gate_product(1, 2 * m - 3)
                                if m == 3:
                                    sum_abs(1)
                                if m == 4:
                                    gate_turn(1)


_INS = ["x", "ctx_4096", "L0_xattn_x1_scale", "L0_xattn_x1_zp", "L0_xattn_x2_scale", "L0_xattn_x2_zp",
        "L0_ffn_gate_w", "L0_ffn_gate_b", "L0_ffn_w1", "L0_ffn_b1", "L0_ffn_w2", "L0_ffn_b2"]


def kernel(**inputs):
    import numpy as np
    import concourse.bacc as bacc
    from concourse.bass_utils import run_bass_kernel_spmd

    nc = bacc.Bacc("TRN2", target_bir_lowering=False, num_devices=1)
    arrays, args = {}, []
    for name in _INS:
        a = np.ascontiguousarray(inputs[name])
        arrays[f"in_{name}_dram"] = a
        args.append(nc.dram_tensor(f"in_{name}_dram", a.shape, mybir.dt.from_np(a.dtype), kind="ExternalInput").ap())
    out = nc.dram_tensor("out_0_dram", (B, S, D), F32, kind="ExternalOutput").ap()
    build(nc, *args, out)
    r = run_bass_kernel_spmd(nc, [arrays], core_ids=[0])
    return r.results[0]["out_0_dram"]
```
